# Optimizing a Trainium2 kernel written in Bass

```python
import numpy as np
import jax
import jax.numpy as jnp

def _softmax(x, axis=-1):
    return jax.nn.softmax(x, axis=axis)

def _gelu(x):
    return jax.nn.gelu(x, approximate=True)

def _silu(x):
    return jax.nn.silu(x)

def _sigmoid(x):
    return jax.nn.sigmoid(x)

def _layernorm(x, axis=-1, eps=1e-05):
    m = jnp.mean(x, axis=axis, keepdims=True)
    v = jnp.var(x, axis=axis, keepdims=True)
    return (x - m) / jnp.sqrt(v + eps)

def _scatter_add(tgt, idx, src, axis=0):
    return tgt.at[idx].add(src)

def _segment_sum(src, seg, n):
    return jax.ops.segment_sum(src, seg, n)
kernel_name = 'mk_adj_resnorm_d2_adj_r2_05a495'

def setup_inputs(seed: int=0):
    np.random.seed(seed)
    _w = jnp.asarray

    def _rec_inputs():
        import jax
        import jax.numpy as jnp
        _gk = jax.random.key(seed)
        x = -0.000125 + 0.9999 * jax.random.normal(jax.random.fold_in(_gk, 1), (64, 128, 128), jnp.float32)
        _w = (1.0 + jnp.arange(128, dtype=jnp.float32)) ** (-0.5)
        _w = _w / _w.mean()
        _pij = jnp.clip(0.015625 * _w[:, None] * _w[None, :], 0.0, 1.0)
        _a = jax.random.uniform(jax.random.fold_in(_gk, 2), (128, 128)) < _pij
        _a = jnp.logical_or(_a, jnp.swapaxes(_a, -1, -2))
        _a = jnp.logical_or(_a, jnp.eye(128, dtype=bool))
        _af = _a.astype(jnp.float32)
        _af = _af * jax.random.uniform(jax.random.fold_in(_gk, 3), (128, 128), jnp.float32, 0.05, 0.000488281)
        adj = _af
        return (x, adj)
    x, adj = _rec_inputs()

    def _L0_gnn_setup():
        import jax, jax.numpy as jnp
        import numpy as np
        B, T, D, H = (64, 1024, 128, 128)
        MAX_SKIP = 4

        def _lstm_last(Wih, Whh, bih, bhh, xs):
            N, _, Hd = xs.shape
            bias = bih + bhh

            def step(carry, x_t):
                h, c = carry
                g = x_t @ Wih.T + h @ Whh.T + bias
                i, f, gg, o = jnp.split(g, 4, axis=-1)
                c = jax.nn.sigmoid(f) * c + jax.nn.sigmoid(i) * jnp.tanh(gg)
                h = jax.nn.sigmoid(o) * jnp.tanh(c)
                return ((h, c), None)
            init = (jnp.zeros((N, Hd), xs.dtype), jnp.zeros((N, Hd), xs.dtype))
            (h_last, _), _ = jax.lax.scan(step, init, jnp.swapaxes(xs, 0, 1))
            return h_last
        key = jax.random.key(seed)
        ks = jax.random.split(key, 8)
        s = 0.05
        x = jax.random.normal(ks[0], (B, T, D), jnp.float32)
        adj = jax.random.uniform(ks[1], (T, T), jnp.float32) / T
        Wg0 = jax.random.normal(ks[2], (D, H), jnp.float32) * s
        bg0 = jnp.zeros((H,), jnp.float32)
        Wg1 = jax.random.normal(ks[3], (H, H), jnp.float32) * s
        bg1 = jnp.zeros((H,), jnp.float32)
        Wih = jax.random.normal(ks[4], (MAX_SKIP, 4 * H, H), jnp.float32) * s
        Whh = jax.random.normal(ks[5], (MAX_SKIP, 4 * H, H), jnp.float32) * s
        bih = jax.random.normal(ks[6], (MAX_SKIP, 4 * H), jnp.float32) * s
        bhh = jax.random.normal(ks[7], (MAX_SKIP, 4 * H), jnp.float32) * s
        return dict(x=x, adj=adj, Wg0=Wg0, bg0=bg0, Wg1=Wg1, bg1=bg1, Wih=Wih, Whh=Whh, bih=bih, bhh=bhh)
    _L0_gnn_all = _L0_gnn_setup()
    _L0_gnn_in = {k: v for k, v in _L0_gnn_all.items() if k in ('Wg0', 'bg0', 'Wg1', 'bg1', 'Wih', 'Whh', 'bih', 'bhh')}
    del _L0_gnn_all

    def _L1_gnn_setup():
        import jax, jax.numpy as jnp
        import numpy as np
        EPS = 1e-05

        def _batchnorm(x, gamma, beta):
            mu = jnp.mean(x, axis=0)
            var = jnp.var(x, axis=0)
            return (x - mu) * jax.lax.rsqrt(var + EPS) * gamma + beta
        key = jax.random.key(seed)
        ks = jax.random.split(key, 4)
        b, n, d, h, o = (32, 1024, 128, 256, 128)
        features = jax.random.normal(ks[0], (b, n, d), dtype=jnp.float32)
        A = jax.random.uniform(ks[1], (n, n), dtype=jnp.float32)
        lim1 = float(np.sqrt(6.0 / (d + h)))
        W1 = jax.random.uniform(ks[2], (h, d), minval=-lim1, maxval=lim1, dtype=jnp.float32)
        b1 = jnp.zeros((h,), jnp.float32)
        lim2 = float(np.sqrt(6.0 / (h + o)))
        W2 = jax.random.uniform(ks[3], (o, h), minval=-lim2, maxval=lim2, dtype=jnp.float32)
        b2 = jnp.zeros((o,), jnp.float32)
        g1 = jnp.ones((h,), jnp.float32)
        be1 = jnp.zeros((h,), jnp.float32)
        g2 = jnp.ones((o,), jnp.float32)
        be2 = jnp.zeros((o,), jnp.float32)
        return {'features': features, 'A': A, 'W1': W1, 'b1': b1, 'g1': g1, 'be1': be1, 'W2': W2, 'b2': b2, 'g2': g2, 'be2': be2}
    _L1_gnn_all = _L1_gnn_setup()
    _L1_gnn_in = {k: v for k, v in _L1_gnn_all.items() if k in ('W1', 'b1', 'g1', 'be1', 'W2', 'b2', 'g2', 'be2')}
    del _L1_gnn_all
    return {'x': x, 'adj': adj, 'L0_gnn_Wg0': _L0_gnn_in['Wg0'], 'L0_gnn_bg0': _L0_gnn_in['bg0'], 'L0_gnn_Wg1': _L0_gnn_in['Wg1'], 'L0_gnn_bg1': _L0_gnn_in['bg1'], 'L0_gnn_Wih': _L0_gnn_in['Wih'], 'L0_gnn_Whh': _L0_gnn_in['Whh'], 'L0_gnn_bih': _L0_gnn_in['bih'], 'L0_gnn_bhh': _L0_gnn_in['bhh'], 'L1_gnn_W1': _L1_gnn_in['W1'], 'L1_gnn_b1': _L1_gnn_in['b1'], 'L1_gnn_g1': _L1_gnn_in['g1'], 'L1_gnn_be1': _L1_gnn_in['be1'], 'L1_gnn_W2': _L1_gnn_in['W2'], 'L1_gnn_b2': _L1_gnn_in['b2'], 'L1_gnn_g2': _L1_gnn_in['g2'], 'L1_gnn_be2': _L1_gnn_in['be2']}

def reference(x, adj, L0_gnn_Wg0, L0_gnn_bg0, L0_gnn_Wg1, L0_gnn_bg1, L0_gnn_Wih, L0_gnn_Whh, L0_gnn_bih, L0_gnn_bhh, L1_gnn_W1, L1_gnn_b1, L1_gnn_g1, L1_gnn_be1, L1_gnn_W2, L1_gnn_b2, L1_gnn_g2, L1_gnn_be2):
    import jax
    import jax.numpy as jnp

    def _L0_gnn_ref(x, adj, Wg0, bg0, Wg1, bg1, Wih, Whh, bih, bhh):
        import jax, jax.numpy as jnp
        import numpy as np
        B, T, D, H = (64, 1024, 128, 128)
        MAX_SKIP = 4

        def _lstm_last(Wih, Whh, bih, bhh, xs):
            N, _, Hd = xs.shape
            bias = bih + bhh

            def step(carry, x_t):
                h, c = carry
                g = x_t @ Wih.T + h @ Whh.T + bias
                i, f, gg, o = jnp.split(g, 4, axis=-1)
                c = jax.nn.sigmoid(f) * c + jax.nn.sigmoid(i) * jnp.tanh(gg)
                h = jax.nn.sigmoid(o) * jnp.tanh(c)
                return ((h, c), None)
            init = (jnp.zeros((N, Hd), xs.dtype), jnp.zeros((N, Hd), xs.dtype))
            (h_last, _), _ = jax.lax.scan(step, init, jnp.swapaxes(xs, 0, 1))
            return h_last
        h = jax.nn.relu(jnp.einsum('ts,bsh->bth', adj, x @ Wg0 + bg0))
        h = jax.nn.relu(jnp.einsum('ts,bsh->bth', adj, h @ Wg1 + bg1))
        Bv, Tv, Hd = h.shape
        for p in range(1, MAX_SKIP + 1):
            nw = Tv // p
            wins = h[:, :nw * p, :].reshape(Bv * nw, p, Hd)
            last = _lstm_last(Wih[p - 1], Whh[p - 1], bih[p - 1], bhh[p - 1], wins)
            idx = jnp.arange(nw) * p + (p - 1)
            h = h.at[:, idx, :].set(last.reshape(Bv, nw, Hd))
        return h

    def _L1_gnn_ref(features, A, W1, b1, g1, be1, W2, b2, g2, be2):
        import jax, jax.numpy as jnp
        import numpy as np
        EPS = 1e-05

        def _batchnorm(x, gamma, beta):
            mu = jnp.mean(x, axis=0)
            var = jnp.var(x, axis=0)
            return (x - mu) * jax.lax.rsqrt(var + EPS) * gamma + beta
        b, n, d = features.shape
        A_norm = A + jnp.eye(n, dtype=A.dtype)
        deg = jnp.sum(A_norm, axis=0) + jnp.sum(A_norm, axis=1) - jnp.diagonal(A_norm)
        dinv = jax.lax.rsqrt(deg)
        A_hat = A_norm * dinv[:, None] * dinv[None, :]
        agg = jnp.einsum('nm,bmd->bnd', A_hat, features)
        x = agg.reshape(-1, d)
        h = jax.nn.relu(_batchnorm(x @ W1.T + b1, g1, be1))
        out = h @ W2.T + b2
        out = _batchnorm(out, g2, be2)
        return out.reshape(b, n, -1)
    x = _layernorm(x + _L0_gnn_ref(x, adj, L0_gnn_Wg0, L0_gnn_bg0, L0_gnn_Wg1, L0_gnn_bg1, L0_gnn_Wih, L0_gnn_Whh, L0_gnn_bih, L0_gnn_bhh), axis=-1)
    x = _layernorm(x + _L1_gnn_ref(x, adj, L1_gnn_W1, L1_gnn_b1, L1_gnn_g1, L1_gnn_be1, L1_gnn_W2, L1_gnn_b2, L1_gnn_g2, L1_gnn_be2), axis=-1)
    return x

_drawn_inputs = setup_inputs


def setup_inputs(seed=0):
    import zlib

    import numpy as np

    out = dict(_drawn_inputs(seed))
    spreads = {'L0_gnn_bg0': (0.0, 0.8),
     'L0_gnn_bg1': (0.0, 0.8),
     'L1_gnn_b1': (0.0, 0.8),
     'L1_gnn_g1': (1.0, 0.2),
     'L1_gnn_be1': (0.0, 0.1),
     'L1_gnn_b2': (0.0, 0.8),
     'L1_gnn_g2': (1.0, 0.2),
     'L1_gnn_be2': (0.0, 0.1)}
    factors = {'L0_gnn_Wg0': 8.0,
     'L0_gnn_Wg1': 8.0,
     'L0_gnn_Wih': 8.0,
     'L0_gnn_Whh': 8.0,
     'L0_gnn_bih': 2.767,
     'L0_gnn_bhh': 2.801}
    for name, (base, spread) in spreads.items():
        noise = np.random.default_rng([zlib.crc32(name.encode()), seed]).standard_normal(out[name].shape)
        drawn = base * np.exp(spread * noise) if base else spread * noise
        out[name] = jnp.asarray(drawn.astype(out[name].dtype))
    for name, factor in factors.items():
        out[name] = (out[name] * factor).astype(out[name].dtype)
    return out
```

```python
import concourse.bass as bass
from concourse import mybir
from concourse.alu_op_type import AluOpType as ALU
from contextlib import ExitStack

F32 = mybir.dt.float32
F32R = mybir.dt.float32r
ACT = mybir.ActivationFunctionType
AX = mybir.AxisListType

B, T, D = 64, 128, 128
HID = 256
HALVES = HID // D
GATES = 4
I, F, G, O = range(GATES)
SKIPS = 4
NB = 4
COLS = NB * T
SLOTS = 2
ITERS = B // (NB * SLOTS)
EPS = 1e-5
FREE, READY = 1, 2
FUNCS = {I: ACT.Sigmoid, F: ACT.Sigmoid, G: ACT.Tanh, O: ACT.Sigmoid}

ROW_BIH, ROW_BHH = 0, SKIPS * GATES
ROW_BG0 = 2 * SKIPS * GATES
ROW_B1 = ROW_BG0 + 1
ROW_G1 = ROW_B1 + HALVES
ROW_BE1 = ROW_G1 + HALVES
ROW_B2 = ROW_BE1 + HALVES
ROW_G2 = ROW_B2 + 1
ROW_BE2 = ROW_G2 + 1
NROWS = ROW_BE2 + 1


def lstm_plan(p):
    windows = T // p
    per_chunk = 8 if windows % 16 == 0 else 7
    return per_chunk, windows // (per_chunk * SLOTS)


def gates_of(step):
    return [I, G, O] if step == 0 else [I, G, F, O]


def build(nc, x, adj, Wg0, bg0, Wg1, bg1, Wih, Whh, bih, bhh, W1, b1, g1, be1, W2, b2, g2, be2, out):
    x_v = x.rearrange("b t d -> t b d")
    out_v = out.rearrange("b t d -> t b d")
    kept = ExitStack()
    with kept:
        def sb(name, shape, dt=F32, where=kept):
            return where.enter_context(nc.sbuf_tensor(name, shape, dt))

        def sem(name):
            return kept.enter_context(nc.semaphore(name))

        H_hi = sb("H_hi", [128, T, B], F32R)
        H_lo = sb("H_lo", [128, T, B], F32R)
        ident = sb("ident", [128, 128])
        a_hatT = sb("a_hatT", [128, T])
        w1T = sb("w1T", [128, HALVES, D])
        w2T = sb("w2T", [128, HALVES, D])
        cols = sb("cols", [128, NROWS])
        gate_bias = sb("gate_bias", [128, SKIPS * GATES])
        bank = [kept.enter_context(nc.psum_tensor(f"bank{n}", [128, COLS], F32)) for n in range(8)]

        lstm_mem = ExitStack()
        w_hi = [[sb(f"w_hi{p}{k}", [128, GATES, D], F32R, lstm_mem) for k in range(2)] for p in range(SKIPS)]
        w_lo = [[sb(f"w_lo{p}{k}", [128, GATES, D], F32R, lstm_mem) for k in range(2)] for p in range(SKIPS)]

        gnn_mem = ExitStack()
        first_gnn(nc, sb, sem, gnn_mem, bank, x_v, adj, Wg0, bg0, Wg1, bg1, Wih, Whh, bih, bhh, W1, b1, g1, be1,
                  W2, b2, g2, be2, H_hi, H_lo, ident, a_hatT, w1T, w2T, cols, gate_bias, w_hi, w_lo)
        gnn_mem.close()
        lstms(nc, sb, sem, lstm_mem, bank, H_hi, H_lo, gate_bias, w_hi, w_lo)
        lstm_mem.close()
        second_gnn(nc, sb, sem, kept, bank, x_v, out_v, H_hi, H_lo, ident, a_hatT, w1T, w2T, cols)


def first_gnn(nc, sb, sem, mem, bank, x_v, adj, Wg0, bg0, Wg1, bg1, Wih, Whh, bih, bhh, W1, b1, g1, be1,
              W2, b2, g2, be2, H_hi, H_lo, ident, a_hatT, w1T, w2T, cols, gate_bias, w_hi, w_lo):
    def tile(name, shape, dt=F32):
        return sb(name, shape, dt, mem)

    adj_sb = tile("adj_sb", [128, T])
    adjT = tile("adjT", [128, T])
    a_norm = tile("a_norm", [128, T])
    a_normT = tile("a_normT", [128, T])
    a_diag = tile("a_diag", [128, T])
    a_half = tile("a_half", [128, T])
    degs = tile("degs", [128, 8])
    wg0 = tile("wg0", [128, D])
    wg1 = tile("wg1", [128, D])
    bg1_row = tile("bg1_row", [1, D])
    bg1_all = tile("bg1_all", [128, 1, D])
    ones = tile("ones", [128, 128])
    agg_bias = tile("agg_bias", [128, 1, T])
    rows = tile("rows", [NROWS, D])
    w1_nat = tile("w1_nat", [128, HALVES, D])
    w2_nat = tile("w2_nat", [128, HALVES, D])
    w_nat = [[tile(f"w_nat{n}{k}", [128, GATES, D]) for k in range(2)] for n in range(2)]
    xs = [tile(f"xs{k}", [128, NB, D]) for k in range(SLOTS)]
    agg = [tile(f"agg{k}", [128, COLS]) for k in range(SLOTS)]
    pre1 = [tile(f"pre1{k}", [128, NB, T]) for k in range(SLOTS)]
    h1 = [tile(f"h1{k}", [128, NB, T]) for k in range(SLOTS)]
    z2 = [tile(f"z2{k}", [128, NB, D]) for k in range(SLOTS)]

    adj_in, small_in, rows_in = sem("adj_in"), sem("small_in"), sem("rows_in")
    w_in = [[sem(f"w_in{n}{k}") for k in range(2)] for n in range(2)]
    ident_zero, ident_made = sem("ident_zero"), sem("ident_made")
    ones_made = sem("ones_made")
    prep_t = sem("prep_t")
    prep_hi = sem("prep_hi")
    prep_lo = sem("prep_lo")
    dve_prep = sem("dve_prep")
    act_prep = sem("act_prep")
    root_out = sem("root_out")
    x_in = [sem(f"x_in{k}") for k in range(SLOTS)]
    agg_made = [sem(f"agg_made{k}") for k in range(SLOTS)]
    agg_out = [sem(f"agg_out{k}") for k in range(SLOTS)]
    pre1_made = [sem(f"pre1_made{k}") for k in range(SLOTS)]
    pre1_out = [sem(f"pre1_out{k}") for k in range(SLOTS)]
    h1_out = [sem(f"h1_out{k}") for k in range(SLOTS)]
    z2_made = [sem(f"z2_made{k}") for k in range(SLOTS)]
    z2_out = [sem(f"z2_out{k}") for k in range(SLOTS)]
    h2_made = [sem(f"h2_made{k}") for k in range(SLOTS)]
    hi_out = [sem(f"hi_out{k}") for k in range(SLOTS)]
    lo_out = [sem(f"lo_out{k}") for k in range(SLOTS)]

    GROUPS = [(p, k) for p in range(SKIPS) for k in range(2)]
    P_ADJ, P_ROWS, P_W, P_HAT, P_LSTM = 1, 2, 3, 4, 5
    n_small = 5

    with nc.Block() as block:
        @block.sync
        def _(sp):
            sp.dma_start(adj_sb[:, :], adj).then_inc(adj_in, 16)
            sp.dma_start(wg0[:, :], Wg0).then_inc(small_in, 16)
            sp.dma_start(wg1[:, :], Wg1).then_inc(small_in, 16)
            sp.dma_start(bg1_row[:, :], bg1.rearrange("(o d) -> o d", o=1)).then_inc(small_in, 16)
            sp.dma_start(w1_nat[:, :, :], W1.rearrange("(n h) d -> h n d", n=HALVES)).then_inc(small_in, 16)
            sp.dma_start(w2_nat[:, :, :], W2.rearrange("o (n h) -> o n h", n=HALVES)).then_inc(small_in, 16)
            with sp.Fori(0, ITERS) as i:
                for k in range(SLOTS):
                    sp.wait_ge(agg_made[k], i + FREE)
                    sp.dma_start(xs[k][:, :, :], x_v[:, bass.ds(i * (SLOTS * NB) + k * NB, NB), :]).then_inc(x_in[k], 16)

        @block.gpsimd
        def _(pool):
            for counters in (agg_made, agg_out, pre1_made, pre1_out, h1_out, z2_made, z2_out, h2_made, hi_out, lo_out):
                for k in range(SLOTS):
                    pool.sem_inc(counters[k], FREE)
            nc.gpsimd.memset(ident[:, :], 0.0).then_inc(ident_zero, 1)
            nc.gpsimd.memset(ones[:, :], 1.0).then_inc(ones_made, 1)
            pool.wait_ge(ident_zero, 1)
            nc.gpsimd.affine_select(out=ident[:, :], in_=ident[:, :], compare_op=ALU.not_equal, fill=1.0, base=0,
                                    pattern=[[-1, 128]], channel_multiplier=1).then_inc(ident_made, 1)

        @block.tensor
        def _(pe):
            pe.wait_ge(adj_in, 16)
            pe.wait_ge(ident_made, 1)
            nc.tensor.transpose(bank[0][:, 0:T], adj_sb[:, :], ident[:, :])
            pe.wait_ge(small_in, 16 * n_small)
            pe.wait_ge(ones_made, 1)
            nc.tensor.matmul(bank[0][:, 128:256], ones[0:1, :], bg1_row[:, :], start=True, stop=True)
            pe.wait_ge(dve_prep, 1)
            nc.tensor.transpose(bank[0][:, 256:384], a_norm[:, :], ident[:, :]).then_inc(prep_t, 1)
            pe.wait_ge(rows_in, 16 * 9)
            nc.tensor.transpose(bank[1][:, 0:NROWS], rows[:, :], ident[0:NROWS, 0:NROWS])
            pe.wait_ge(act_prep, 1)
            nc.tensor.matmul(bank[1][:, 128:256], ones[:, :], adjT[:, :], start=True, stop=True).then_inc(prep_t, 1)
            for n in range(HALVES):
                nc.tensor.transpose(bank[2][:, n * D:(n + 1) * D], w1_nat[:, n, :], ident[:, :])
            for n in range(HALVES):
                last = nc.tensor.transpose(bank[2][:, (2 + n) * D:(3 + n) * D], w2_nat[:, n, :], ident[:, :])
            last.then_inc(prep_t, 1)
            pe.wait_ge(dve_prep, 7)
            nc.tensor.transpose(bank[3][:, 0:T], a_half[:, :], ident[:, :]).then_inc(prep_t, 1)
            for n, (p, k) in enumerate(GROUPS):
                pe.wait_ge(w_in[p % 2][k], 16 * (p // 2 + 1))
                if n >= 4:
                    pe.wait_ge(prep_lo, n - 3)
                for g in range(GATES):
                    last = nc.tensor.transpose(bank[4 + n % 4][:, g * D:(g + 1) * D], w_nat[p % 2][k][:, g, :], ident[:, :])
                last.then_inc(prep_t, 1)
            pe.wait_ge(dve_prep, 9)
            pe.wait_ge(prep_lo, len(GROUPS))
            with pe.Fori(0, ITERS) as i:
                for k in range(SLOTS):
                    pe.wait_ge(x_in[k], i * 16 + 16)
                    pe.wait_ge(agg_out[k], i + FREE)
                    for b in range(NB):
                        last = nc.tensor.matmul(bank[k][:, b * T:(b + 1) * T], xs[k][:, b, :], adjT[:, :], start=True, stop=True)
                    last.then_inc(agg_made[k], 1)
                for k in range(SLOTS):
                    pe.wait_ge(agg_out[k], i + READY)
                    pe.wait_ge(pre1_out[k], i + FREE)
                    nc.tensor.matmul(bank[2 + k][:, :], wg0[:, :], agg[k][:, :], start=True, stop=True).then_inc(pre1_made[k], 1)
                for k in range(SLOTS):
                    pe.wait_ge(h1_out[k], i + READY)
                    pe.wait_ge(z2_out[k], i + FREE)
                    for b in range(NB):
                        last = nc.tensor.matmul(bank[4 + k][:, b * D:(b + 1) * D], h1[k][:, b, :], wg1[:, :], start=True, stop=True)
                    last.then_inc(z2_made[k], 1)
                for k in range(SLOTS):
                    pe.wait_ge(z2_out[k], i + READY)
                    pe.wait_ge(lo_out[k], i + FREE)
                    for b in range(NB):
                        last = nc.tensor.matmul(bank[6 + k][:, b * T:(b + 1) * T], z2[k][:, b, :], adjT[:, :], start=True, stop=True)
                    last.then_inc(h2_made[k], 1)

        @block.scalar
        def _(act):
            for n in range(2):
                for k, w in enumerate((Wih, Whh)):
                    act.dma_start(w_nat[n][k][:, :, :], w[n].rearrange("(g h) d -> h g d", g=GATES)).then_inc(w_in[n][k], 16)
            act.dma_start(rows[ROW_BIH:ROW_BHH, :], bih.rearrange("p (g h) -> (p g) h", g=GATES)).then_inc(rows_in, 16)
            act.dma_start(rows[ROW_BHH:ROW_BG0, :], bhh.rearrange("p (g h) -> (p g) h", g=GATES)).then_inc(rows_in, 16)
            for row, v, n in ((ROW_BG0, bg0, 1), (ROW_B1, b1, 2), (ROW_G1, g1, 2), (ROW_BE1, be1, 2),
                              (ROW_B2, b2, 1), (ROW_G2, g2, 1), (ROW_BE2, be2, 1)):
                act.dma_start(rows[row:row + n, :], v.rearrange("(n h) -> n h", n=n)).then_inc(rows_in, 16)
            act.wait_ge(prep_t, P_ADJ)
            nc.scalar.copy(adjT[:, :], bank[0][:, 0:T]).then_inc(act_prep, 1)
            nc.scalar.copy(bg1_all[:, 0, :], bank[0][:, 128:256])
            nc.scalar.copy(a_normT[:, :], bank[0][:, 256:384]).then_inc(act_prep, 1)
            act.wait_ge(dve_prep, 5)
            nc.scalar.activation(degs[:, 6:7], degs[:, 4:5], ACT.Sqrt).then_inc(root_out, 1)
            act.wait_ge(prep_t, P_W)
            nc.scalar.copy(w1T[:, :, :], bank[2][:, 0:2 * D].rearrange("p (n d) -> p n d", n=2))
            nc.scalar.copy(w2T[:, :, :], bank[2][:, 2 * D:4 * D].rearrange("p (n d) -> p n d", n=2)).then_inc(act_prep, 1)
            for n, (p, k) in enumerate(GROUPS):
                act.wait_ge(prep_t, P_LSTM + n)
                nc.scalar.copy(w_hi[p][k][:, :, :], bank[4 + n % 4][:, :].rearrange("p (g d) -> p g d", g=GATES)).then_inc(prep_hi, 1)
                if p < 2:
                    w = (Wih, Whh)[k]
                    act.dma_start(w_nat[p % 2][k][:, :, :], w[p + 2].rearrange("(g h) d -> h g d", g=GATES)).then_inc(w_in[p % 2][k], 16)
            with act.Fori(0, ITERS) as i:
                for k in range(SLOTS):
                    act.wait_ge(agg_made[k], i + READY)
                    act.wait_ge(pre1_made[k], i + FREE)
                    nc.scalar.copy(agg[k][:, :], bank[k][:, :]).then_inc(agg_out[k], 1)
                for k in range(SLOTS):
                    act.wait_ge(pre1_out[k], i + READY)
                    act.wait_ge(z2_made[k], i + FREE)
                    nc.scalar.activation(h1[k][:, :, :], pre1[k][:, :, :], ACT.Relu).then_inc(h1_out[k], 1)
                for k in range(SLOTS):
                    act.wait_ge(h2_made[k], i + READY)
                    nc.scalar.activation(H_hi[:, :, bass.ds(i * (SLOTS * NB) + k * NB, NB)],
                                         bank[6 + k][:, :].rearrange("p (b t) -> p t b", b=NB), ACT.Relu).then_inc(hi_out[k], 1)

        @block.vector
        def _(dve):
            done = [0]

            def step(ins):
                done[0] += 1
                ins.then_inc(dve_prep, 1)
                dve.wait_ge(dve_prep, done[0])

            dve.wait_ge(adj_in, 16)
            dve.wait_ge(ident_made, 1)
            step(nc.vector.tensor_tensor(a_norm[:, :], adj_sb[:, :], ident[:, :], ALU.add))
            step(nc.vector.tensor_tensor(a_diag[:, :], a_norm[:, :], ident[:, :], ALU.mult))
            nc.vector.reduce_sum(degs[:, 0:1], a_norm[:, :], AX.X)
            nc.vector.reduce_sum(degs[:, 2:3], a_diag[:, :], AX.X)
            dve.wait_ge(act_prep, 2)
            step(nc.vector.reduce_sum(degs[:, 1:2], a_normT[:, :], AX.X))
            step(nc.vector.tensor_tensor(degs[:, 3:4], degs[:, 0:1], degs[:, 1:2], ALU.add))
            step(nc.vector.tensor_tensor(degs[:, 4:5], degs[:, 3:4], degs[:, 2:3], ALU.subtract))
            dve.wait_ge(root_out, 1)
            step(nc.vector.reciprocal(degs[:, 5:6], degs[:, 6:7]))
            step(nc.vector.tensor_scalar(a_half[:, :], a_norm[:, :], degs[:, 5:6], None, ALU.mult))
            dve.wait_ge(prep_t, P_ROWS)
            step(nc.vector.tensor_copy(cols[:, :], bank[1][:, 0:NROWS]))
            nc.vector.tensor_tensor(gate_bias[:, :], cols[:, ROW_BIH:ROW_BHH], cols[:, ROW_BHH:ROW_BG0], ALU.add)
            nc.vector.tensor_scalar(agg_bias[:, 0, :], bank[1][:, 128:256], cols[:, ROW_BG0:ROW_BG0 + 1], None, ALU.mult)
            dve.wait_ge(prep_t, P_HAT)
            step(nc.vector.tensor_scalar(a_hatT[:, :], bank[3][:, 0:T], degs[:, 5:6], None, ALU.mult))
            for n, (p, k) in enumerate(GROUPS):
                dve.wait_ge(prep_hi, n + 1)
                nc.vector.tensor_tensor(w_lo[p][k][:, :, :], bank[4 + n % 4][:, :].rearrange("p (g d) -> p g d", g=GATES),
                                        w_hi[p][k][:, :, :].bitcast(F32), ALU.subtract).then_inc(prep_lo, 1)
            dve.wait_ge(act_prep, 3)
            with dve.Fori(0, ITERS) as i:
                for k in range(SLOTS):
                    dve.wait_ge(pre1_made[k], i + READY)
                    dve.wait_ge(h1_out[k], i + FREE)
                    nc.vector.tensor_tensor(pre1[k][:, :, :], bank[2 + k][:, :].rearrange("p (b t) -> p b t", b=NB),
                                            agg_bias[:, :, :].to_broadcast([128, NB, T]), ALU.add).then_inc(pre1_out[k], 1)
                for k in range(SLOTS):
                    dve.wait_ge(z2_made[k], i + READY)
                    dve.wait_ge(h2_made[k], i + FREE)
                    nc.vector.tensor_tensor(z2[k][:, :, :], bank[4 + k][:, :].rearrange("p (b t) -> p b t", b=NB),
                                            bg1_all[:, :, :].to_broadcast([128, NB, D]), ALU.add).then_inc(z2_out[k], 1)
                for k in range(SLOTS):
                    dve.wait_ge(hi_out[k], i + READY)
                    here = bass.ds(i * (SLOTS * NB) + k * NB, NB)
                    nc.vector.scalar_tensor_tensor(out=H_lo[:, :, here], in0=bank[6 + k][:, :].rearrange("p (b t) -> p t b", b=NB),
                                                   scalar=0.0, in1=H_hi[:, :, here].bitcast(F32),
                                                   op0=ALU.max, op1=ALU.subtract).then_inc(lo_out[k], 1)


def lstms(nc, sb, sem, mem, bank, H_hi, H_lo, gate_bias, w_hi, w_lo):
    act_sb = [[sb(f"gate{x}{g}", [128, COLS], F32, mem) for g in range(GATES)] for x in range(SLOTS)]
    cell = [sb(f"cell{x}", [128, COLS], F32, mem) for x in range(SLOTS)]
    cell_in = [sb(f"cell_in{x}", [128, COLS], F32, mem) for x in range(SLOTS)]
    cell_tanh = [sb(f"cell_tanh{x}", [128, COLS], F32, mem) for x in range(SLOTS)]
    state = [sb(f"state{x}", [128, COLS], F32, mem) for x in range(SLOTS)]
    state_hi = [sb(f"state_hi{x}", [128, COLS], F32R, mem) for x in range(SLOTS)]
    state_lo = [sb(f"state_lo{x}", [128, COLS], F32R, mem) for x in range(SLOTS)]

    gates_made = [sem(f"gates_made{x}") for x in range(SLOTS)]
    gates_out = [sem(f"gates_out{x}") for x in range(SLOTS)]
    cell_made = [sem(f"cell_made{x}") for x in range(SLOTS)]
    tanh_out = [sem(f"tanh_out{x}") for x in range(SLOTS)]
    state_out = [sem(f"state_out{x}") for x in range(SLOTS)]
    forgot = [sem(f"forgot{x}") for x in range(SLOTS)]
    split = [sem(f"split{x}") for x in range(SLOTS)]

    plan = []
    base = dict(gates=FREE, steps=FREE)
    for p in range(1, SKIPS + 1):
        per_chunk, iters = lstm_plan(p)
        per = dict(gates=len(gates_of(0)) + GATES * (p - 1), steps=p)
        plan.append((p, per_chunk, iters, dict(base), per))
        for key in base:
            base[key] += iters * per[key]

    def positions(buf, i, p, per_chunk, x, step):
        first = i * (SLOTS * per_chunk) + x * per_chunk
        grouped = buf[:, 0:T // p * p, :].rearrange("d (w s) b -> d w s b", s=p)
        return grouped[:, bass.ds(first, per_chunk), step, :]

    def earlier(i, p):
        covered, read = (SLOTS * lstm_plan(q)[0] * q for q in (p - 1, p))
        return [i * (read // covered) + -(-read // covered), lstm_plan(p - 1)[1]]

    with nc.Block() as block:
        @block.gpsimd
        def _(pool):
            for counters in (gates_made, gates_out, cell_made, tanh_out, state_out, forgot, split):
                for x in range(SLOTS):
                    pool.sem_inc(counters[x], FREE)

        @block.tensor
        def _(pe):
            for p, per_chunk, iters, at, per in plan:
                n = per_chunk * B
                with pe.Fori(0, iters) as i:
                    gate_no = [0] * SLOTS
                    for step in range(p):
                        for x in range(SLOTS):
                            if step == 0 and x == 0 and p > 1:
                                _, _, _, at0, per0 = plan[p - 2]
                                reach, _ = earlier(i, p)
                                for y in range(SLOTS):
                                    pe.wait_ge(state_out[y], reach * per0["steps"] + at0["steps"])
                            pe.wait_ge(gates_out[x], i * per["gates"] + (at["gates"] + gate_no[x]))
                            gates = gates_of(step)
                            in_hi = positions(H_hi, i, p, per_chunk, x, step)
                            in_lo = positions(H_lo, i, p, per_chunk, x, step)
                            for g in gates:
                                ps = bank[x * GATES + g][:, 0:n]
                                nc.tensor.matmul(ps, w_hi[p - 1][0][:, g, :], in_hi, start=True, stop=False)
                                nc.tensor.matmul(ps, w_hi[p - 1][0][:, g, :], in_lo, start=False, stop=False)
                                last = nc.tensor.matmul(ps, w_lo[p - 1][0][:, g, :], in_hi, start=False, stop=step == 0)
                                if step == 0:
                                    last.then_inc(gates_made[x], 1)
                            if step > 0:
                                pe.wait_ge(state_out[x], i * per["steps"] + (at["steps"] + step))
                                for g in gates:
                                    ps = bank[x * GATES + g][:, 0:n]
                                    nc.tensor.matmul(ps, w_hi[p - 1][1][:, g, :], state_hi[x][:, 0:n], start=False, stop=False)
                                    nc.tensor.matmul(ps, w_hi[p - 1][1][:, g, :], state_lo[x][:, 0:n], start=False, stop=False)
                                    nc.tensor.matmul(ps, w_lo[p - 1][1][:, g, :], state_hi[x][:, 0:n],
                                                     start=False, stop=True).then_inc(gates_made[x], 1)
                            gate_no[x] += len(gates)

        @block.scalar
        def _(act):
            for p, per_chunk, iters, at, per in plan:
                n = per_chunk * B
                with act.Fori(0, iters) as i:
                    gate_no = [0] * SLOTS
                    for step in range(p):
                        for x in range(SLOTS):
                            act.wait_ge(state_out[x], i * per["steps"] + (at["steps"] + step))
                            for g in gates_of(step):
                                gate_no[x] += 1
                                act.wait_ge(gates_made[x], i * per["gates"] + (at["gates"] + gate_no[x]))
                                j = (p - 1) * GATES + g
                                nc.scalar.activation(act_sb[x][g][:, 0:n], bank[x * GATES + g][:, 0:n], FUNCS[g],
                                                     bias=gate_bias[:, j:j + 1]).then_inc(gates_out[x], 1)
                            act.wait_ge(cell_made[x], i * per["steps"] + (at["steps"] + step + 1))
                            nc.scalar.activation(cell_tanh[x][:, 0:n], cell[x][:, 0:n], ACT.Tanh).then_inc(tanh_out[x], 1)

        @block.vector
        def _(dve):
            base_forgot = FREE
            for p, per_chunk, iters, at, per in plan:
                n = per_chunk * B
                per_forgot = 2 * (p - 1)
                with dve.Fori(0, iters) as i:
                    gate_no = [0] * SLOTS
                    for step in range(p):
                        for x in range(SLOTS):
                            gate = act_sb[x]
                            first = i * per["gates"] + (at["gates"] + gate_no[x])
                            gate_no[x] += len(gates_of(step))
                            dve.wait_ge(gates_out[x], first + 2)
                            if step == 0:
                                nc.vector.tensor_tensor(cell[x][:, 0:n], gate[I][:, 0:n], gate[G][:, 0:n],
                                                        ALU.mult).then_inc(cell_made[x], 1)
                            else:
                                nc.vector.tensor_tensor(cell_in[x][:, 0:n], gate[I][:, 0:n], gate[G][:, 0:n],
                                                        ALU.mult).then_inc(forgot[x], 1)
                                dve.wait_ge(gates_out[x], first + 3)
                                nc.vector.tensor_tensor(cell[x][:, 0:n], gate[F][:, 0:n], cell[x][:, 0:n],
                                                        ALU.mult).then_inc(forgot[x], 1)
                                dve.wait_ge(forgot[x], i * per_forgot + (base_forgot + 2 * step))
                                nc.vector.tensor_tensor(cell[x][:, 0:n], cell[x][:, 0:n], cell_in[x][:, 0:n],
                                                        ALU.add).then_inc(cell_made[x], 1)
                            dve.wait_ge(gates_out[x], first + len(gates_of(step)))
                            dve.wait_ge(tanh_out[x], i * per["steps"] + (at["steps"] + step + 1))
                            nc.vector.tensor_tensor(state[x][:, 0:n], gate[O][:, 0:n], cell_tanh[x][:, 0:n],
                                                    ALU.mult).then_inc(split[x], 1)
                            if step == p - 1:
                                to_hi = positions(H_hi, i, p, per_chunk, x, step)
                                to_lo = positions(H_lo, i, p, per_chunk, x, step)
                                st = state[x][:, 0:n].rearrange("p (w b) -> p w b", b=B)
                            else:
                                to_hi, to_lo, st = state_hi[x][:, 0:n], state_lo[x][:, 0:n], state[x][:, 0:n]
                            done = i * (2 * per["steps"]) + 2 * (at["steps"] - FREE + step) + FREE
                            dve.wait_ge(split[x], done + 1)
                            nc.vector.tensor_copy(to_hi, st).then_inc(split[x], 1)
                            dve.wait_ge(split[x], done + 2)
                            nc.vector.tensor_tensor(to_lo, st, to_hi.bitcast(F32), ALU.subtract).then_inc(state_out[x], 1)
                base_forgot += iters * per_forgot


def second_gnn(nc, sb, sem, mem, bank, x_v, out_v, H_hi, H_lo, ident, a_hatT, w1T, w2T, cols):
    x1 = sb("x1", [128, B, D])
    hid = [sb(f"hid{n}", [128, B * T]) for n in range(HALVES)]
    o_all = hid[0]
    xr = [sb(f"xr{k}", [128, NB, D]) for k in range(SLOTS)]
    h_sum = [sb(f"h_sum{k}", [128, NB, T]) for k in range(SLOTS)]
    res = [sb(f"res{k}", [128, NB, D]) for k in range(SLOTS)]
    x1s = [sb(f"x1s{k}", [128, NB, D]) for k in range(SLOTS)]
    hh = [sb(f"hh{k}", [128, HALVES, COLS]) for k in range(SLOTS)]
    agg = [hh[k][:, 0, :] for k in range(SLOTS)]
    st = [sb(f"st{k}", [128, NB, 6]) for k in range(SLOTS)]
    sums = [sb(f"sums{k}", [128, NB, 2]) for k in range(SLOTS)]
    diff, sqdiff, mean, var_sum = ([sb(f"{n}{k}", [128, NB, 1]) for k in range(SLOTS)]
                                   for n in ("diff", "sqdiff", "mean", "var_sum"))
    root = [sb(f"root{k}", [128, NB, 1]) for k in range(SLOTS)]
    rstd = [sb(f"rstd{k}", [128, NB, 1]) for k in range(SLOTS)]
    eps = sb("eps", [128, 1])
    broot = sb("broot", [128, 3, 1])
    bst = [sb(f"bst{n}", [128, B // NB, 6]) for n in range(3)]
    bmv = sb("bmv", [128, 3, 2])
    brs = sb("brs", [128, 3, 1])
    scale = sb("scale", [128, 3, 1])
    mshift = sb("mshift", [128, 3, 1])
    shift = sb("shift", [128, 3, 1])

    def per_slot(name):
        return [sem(f"{name}{k}") for k in range(SLOTS)]

    xr_in, hsum_out, hT_made, res_out, x1_out = (per_slot(n) for n in ("xr_in", "hsum_out", "hT_made", "res_out", "x1_out"))
    x1_kept, agg_made, agg_out, hid_made, hid_out, bst_out = (
        per_slot(n) for n in ("x1_kept", "agg2_made", "agg2_out", "hid_made", "hid_out", "bst_out"))
    st_out, ln_part, mv_out, root_out, rstd_out = (
        per_slot(n) for n in ("st_out", "ln_part", "mv_out", "ln_root_out", "rstd_out"))
    eps_made, bn_root = sem("eps_made"), sem("bn_root")
    bn_step = sem("bn_step")
    bn1_done, bn2_done = sem("bn1_done"), sem("bn2_done")
    hh_out, o_made, o_out, ost_out = (per_slot(n) for n in ("hh_out", "o_made", "o_out", "ost_out"))
    y_out, yT_made, res2_out, fin_out, stored = (per_slot(n) for n in ("y_out", "yT_made", "res2_out", "fin_out", "stored"))

    def chunk(i, k):
        return i * (SLOTS * NB) + k * NB

    def ln_stats(dve, k, count, source):
        for b in range(NB):
            last = nc.vector.bn_stats(st[k][:, b, :], source[:, b, :])
        last.then_inc(st_out[k], 1)
        dve.wait_ge(st_out[k], count + READY)
        dve.wait_ge(root_out[k], count + FREE)
        nc.vector.tensor_tensor(sums[k][:, :, :], st[k][:, :, 1:3], st[k][:, :, 4:6], ALU.add)
        nc.vector.tensor_tensor(diff[k][:, :, 0], st[k][:, :, 1], st[k][:, :, 4], ALU.subtract).then_inc(ln_part[k], 1)
        dve.wait_ge(ln_part[k], count * 2 + 1)
        nc.vector.tensor_scalar(mean[k][:, :, 0], sums[k][:, :, 0], 0.5, None, ALU.mult)
        nc.vector.scalar_tensor_tensor(out=sqdiff[k][:, :, 0], in0=diff[k][:, :, 0], scalar=D / 4, in1=diff[k][:, :, 0],
                                       op0=ALU.mult, op1=ALU.mult).then_inc(ln_part[k], 1)
        dve.wait_ge(ln_part[k], count * 2 + 2)
        nc.vector.tensor_tensor(var_sum[k][:, :, 0], sqdiff[k][:, :, 0], sums[k][:, :, 1], ALU.add).then_inc(mv_out[k], 1)

    def ln_finish(dve, k, count, source, target):
        dve.wait_ge(root_out[k], count + READY)
        nc.vector.reciprocal(rstd[k][:, :, 0], root[k][:, :, 0]).then_inc(rstd_out[k], 1)
        dve.wait_ge(rstd_out[k], count + READY)
        for b in range(NB):
            last = nc.vector.tensor_scalar(target[:, b, :], source[:, b, :], mean[k][:, b, 0:1], rstd[k][:, b, 0:1],
                                           ALU.subtract, ALU.mult)
        return last

    def ln_root(act, k, count):
        act.wait_ge(mv_out[k], count + READY)
        act.wait_ge(rstd_out[k], count + FREE)
        nc.scalar.activation(root[k][:, :, 0], var_sum[k][:, :, 0], ACT.Sqrt, bias=eps[:, 0:1], scale=1.0 / D).then_inc(root_out[k], 1)

    def batch_norm(dve, count, which, gain, bias, done):
        lo, hi = which[0], which[-1] + 1
        for n in which:
            last = nc.vector.bn_aggr(bmv[:, n, :], bst[n][:, :, :].rearrange("p c s -> p (c s)"))
        last.then_inc(bn_step, 1)
        dve.wait_ge(bn_root, count // 4 + 1)
        nc.vector.reciprocal(brs[:, lo:hi, 0], broot[:, lo:hi, 0]).then_inc(bn_step, 1)
        dve.wait_ge(bn_step, count + 2)
        nc.vector.tensor_tensor(scale[:, lo:hi, 0], brs[:, lo:hi, 0], gain, ALU.mult).then_inc(bn_step, 1)
        dve.wait_ge(bn_step, count + 3)
        nc.vector.tensor_tensor(mshift[:, lo:hi, 0], bmv[:, lo:hi, 0], scale[:, lo:hi, 0], ALU.mult).then_inc(bn_step, 1)
        dve.wait_ge(bn_step, count + 4)
        nc.vector.tensor_tensor(shift[:, lo:hi, 0], bias, mshift[:, lo:hi, 0], ALU.subtract).then_inc(done, 1)

    with nc.Block() as block:
        @block.sync
        def _(sp):
            with sp.Fori(0, ITERS) as i:
                for k in range(SLOTS):
                    sp.wait_ge(res_out[k], i + FREE)
                    sp.dma_start(xr[k][:, :, :], x_v[:, bass.ds(chunk(i, k), NB), :]).then_inc(xr_in[k], 16)
            with sp.Fori(0, ITERS) as i:
                for k in range(SLOTS):
                    sp.wait_ge(fin_out[k], i + READY)
                    sp.dma_start(out_v[:, bass.ds(chunk(i, k), NB), :], x1s[k][:, :, :]).then_inc(stored[k], 16)
            for k in range(SLOTS):
                sp.wait_ge(stored[k], 16 * ITERS + 16)

        @block.gpsimd
        def _(pool):
            for counters in (hsum_out, hT_made, res_out, x1_out, x1_kept, agg_made, agg_out, hid_made, hid_out, bst_out,
                             st_out, mv_out, root_out, rstd_out, hh_out, o_made, o_out, ost_out, y_out, yT_made,
                             res2_out, fin_out):
                for k in range(SLOTS):
                    pool.sem_inc(counters[k], FREE)
            for k in range(SLOTS):
                pool.sem_inc(stored[k], 16)
            nc.gpsimd.memset(eps[:, :], EPS).then_inc(eps_made, 1)
            with pool.Fori(0, ITERS) as i:
                for k in range(SLOTS):
                    pool.wait_ge(hT_made[k], i + FREE)
                    here = bass.ds(chunk(i, k), NB)
                    nc.gpsimd.tensor_tensor(h_sum[k][:, :, :].rearrange("p b t -> p t b"), H_hi[:, :, here].bitcast(F32),
                                            H_lo[:, :, here].bitcast(F32), ALU.add).then_inc(hsum_out[k], 1)

        @block.tensor
        def _(pe):
            with pe.Fori(0, ITERS) as i:
                for k in range(SLOTS):
                    pe.wait_ge(hsum_out[k], i + READY)
                    pe.wait_ge(res_out[k], i + FREE)
                    for b in range(NB):
                        last = nc.tensor.transpose(bank[k][:, b * D:(b + 1) * D], h_sum[k][:, b, :], ident[:, :])
                    last.then_inc(hT_made[k], 1)
                for k in range(SLOTS):
                    pe.wait_ge(x1_out[k], i + READY)
                    pe.wait_ge(agg_out[k], i + FREE)
                    for b in range(NB):
                        last = nc.tensor.matmul(bank[2 + k][:, b * T:(b + 1) * T], x1s[k][:, b, :], a_hatT[:, :], start=True, stop=True)
                    last.then_inc(agg_made[k], 1)
                for k in range(SLOTS):
                    pe.wait_ge(agg_out[k], i + READY)
                    pe.wait_ge(hid_out[k], i + FREE)
                    for n in range(HALVES):
                        last = nc.tensor.matmul(bank[4 + 2 * k + n][:, :], w1T[:, n, :], agg[k], start=True, stop=True)
                    last.then_inc(hid_made[k], 1)
            with pe.Fori(0, ITERS) as i:
                for k in range(SLOTS):
                    pe.wait_ge(hh_out[k], i + READY)
                    pe.wait_ge(o_out[k], i + FREE)
                    for n in range(HALVES):
                        last = nc.tensor.matmul(bank[k][:, :], w2T[:, n, :], hh[k][:, n, :], start=n == 0, stop=n == HALVES - 1)
                    last.then_inc(o_made[k], 1)
            with pe.Fori(0, ITERS) as i:
                for k in range(SLOTS):
                    pe.wait_ge(y_out[k], i + READY)
                    pe.wait_ge(res2_out[k], i + FREE)
                    for b in range(NB):
                        last = nc.tensor.transpose(bank[2 + k][:, b * D:(b + 1) * D], h_sum[k][:, b, :], ident[:, :])
                    last.then_inc(yT_made[k], 1)

        @block.scalar
        def _(act):
            act.wait_ge(eps_made, 1)
            with act.Fori(0, ITERS) as i:
                for k in range(SLOTS):
                    ln_root(act, k, i)
                for k in range(SLOTS):
                    act.wait_ge(x1_out[k], i + READY)
                    nc.scalar.copy(x1[:, bass.ds(chunk(i, k), NB), :], x1s[k][:, :, :]).then_inc(x1_kept[k], 1)
                for k in range(SLOTS):
                    act.wait_ge(agg_made[k], i + READY)
                    act.wait_ge(hid_made[k], i + FREE)
                    nc.scalar.copy(agg[k], bank[2 + k][:, :]).then_inc(agg_out[k], 1)
                for k in range(SLOTS):
                    act.wait_ge(hid_made[k], i + READY)
                    for n in range(HALVES):
                        last = nc.scalar.activation(hid[n][:, bass.ds(chunk(i, k) * T, COLS)], bank[4 + 2 * k + n][:, :],
                                                    ACT.Identity, bias=cols[:, ROW_B1 + n:ROW_B1 + n + 1])
                    last.then_inc(hid_out[k], 1)
            act.wait_ge(bn_step, 1)
            nc.scalar.activation(broot[:, 0:2, 0], bmv[:, 0:2, 1], ACT.Sqrt, bias=eps[:, 0:1]).then_inc(bn_root, 1)
            act.wait_ge(bn1_done, 1)
            with act.Fori(0, ITERS) as i:
                for k in range(SLOTS):
                    act.wait_ge(o_made[k], i + FREE)
                    for n in range(HALVES):
                        last = nc.scalar.activation(hh[k][:, n, :], hid[n][:, bass.ds(chunk(i, k) * T, COLS)],
                                                    ACT.Relu, bias=shift[:, n, :], scale=scale[:, n, :])
                    last.then_inc(hh_out[k], 1)
            act.wait_ge(bn_step, 5)
            nc.scalar.activation(broot[:, 2:3, 0], bmv[:, 2:3, 1], ACT.Sqrt, bias=eps[:, 0:1]).then_inc(bn_root, 1)
            act.wait_ge(bn2_done, 1)
            with act.Fori(0, ITERS) as i:
                for k in range(SLOTS):
                    act.wait_ge(yT_made[k], i + FREE)
                    nc.scalar.activation(h_sum[k][:, :, :].rearrange("p b t -> p (b t)"), o_all[:, bass.ds(chunk(i, k) * T, COLS)],
                                         ACT.Identity, bias=shift[:, 2, :], scale=scale[:, 2, :]).then_inc(y_out[k], 1)
                for k in range(SLOTS):
                    ln_root(act, k, i + ITERS)

        @block.vector
        def _(dve):
            with dve.Fori(0, ITERS) as i:
                for k in range(SLOTS):
                    dve.wait_ge(hT_made[k], i + READY)
                    dve.wait_ge(xr_in[k], i * 16 + 16)
                    nc.vector.tensor_tensor(res[k][:, :, :], bank[k][:, :].rearrange("p (b d) -> p b d", b=NB),
                                            xr[k][:, :, :], ALU.add).then_inc(res_out[k], 1)
                    dve.wait_ge(res_out[k], i + READY)
                    ln_stats(dve, k, i, res[k])
                for k in range(SLOTS):
                    dve.wait_ge(x1_kept[k], i + FREE)
                    dve.wait_ge(agg_made[k], i + FREE)
                    ln_finish(dve, k, i, res[k], x1s[k]).then_inc(x1_out[k], 1)
                for k in range(SLOTS):
                    dve.wait_ge(hid_out[k], i + READY)
                    for n in range(HALVES):
                        last = nc.vector.bn_stats(bst[n][:, bass.ds(i * SLOTS + k, 1), :].rearrange("p c s -> p (c s)"),
                                                  hid[n][:, bass.ds(chunk(i, k) * T, COLS)])
                    last.then_inc(bst_out[k], 1)
            for k in range(SLOTS):
                dve.wait_ge(bst_out[k], ITERS + FREE)
            batch_norm(dve, 0, [0, 1], cols[:, ROW_G1:ROW_G1 + 2], cols[:, ROW_BE1:ROW_BE1 + 2], bn1_done)
            with dve.Fori(0, ITERS) as i:
                for k in range(SLOTS):
                    dve.wait_ge(o_made[k], i + READY)
                    here = o_all[:, bass.ds(chunk(i, k) * T, COLS)]
                    nc.vector.tensor_scalar(here, bank[k][:, :], cols[:, ROW_B2:ROW_B2 + 1], None, ALU.add).then_inc(o_out[k], 1)
                    dve.wait_ge(o_out[k], i + READY)
                    nc.vector.bn_stats(bst[2][:, bass.ds(i * SLOTS + k, 1), :].rearrange("p c s -> p (c s)"), here).then_inc(ost_out[k], 1)
            for k in range(SLOTS):
                dve.wait_ge(ost_out[k], ITERS + FREE)
            batch_norm(dve, 4, [2], cols[:, ROW_G2:ROW_G2 + 1], cols[:, ROW_BE2:ROW_BE2 + 1], bn2_done)
            for k in range(SLOTS):
                dve.wait_ge(x1_kept[k], ITERS + FREE)
            with dve.Fori(0, ITERS) as i:
                for k in range(SLOTS):
                    dve.wait_ge(yT_made[k], i + READY)
                    nc.vector.tensor_tensor(res[k][:, :, :], bank[2 + k][:, :].rearrange("p (b d) -> p b d", b=NB),
                                            x1[:, bass.ds(chunk(i, k), NB), :], ALU.add).then_inc(res2_out[k], 1)
                    dve.wait_ge(res2_out[k], i + READY)
                    ln_stats(dve, k, i + ITERS, res[k])
                for k in range(SLOTS):
                    dve.wait_ge(stored[k], i * 16 + 16)
                    ln_finish(dve, k, i + ITERS, res[k], x1s[k]).then_inc(fin_out[k], 1)


_INS = ["x", "adj", "L0_gnn_Wg0", "L0_gnn_bg0", "L0_gnn_Wg1", "L0_gnn_bg1", "L0_gnn_Wih", "L0_gnn_Whh", "L0_gnn_bih",
        "L0_gnn_bhh", "L1_gnn_W1", "L1_gnn_b1", "L1_gnn_g1", "L1_gnn_be1", "L1_gnn_W2", "L1_gnn_b2", "L1_gnn_g2",
        "L1_gnn_be2"]


def kernel(**inputs):
    import numpy as _np
    import concourse.bacc as _bacc
    from concourse import mybir as _mybir
    from concourse.bass_utils import run_bass_kernel_spmd as _run

    nc = _bacc.Bacc("TRN2", target_bir_lowering=False, num_devices=1)
    arrays, args = {}, []
    for name in _INS:
        a = _np.ascontiguousarray(inputs[name])
        arrays[f"in_{name}_dram"] = a
        args.append(nc.dram_tensor(f"in_{name}_dram", a.shape, _mybir.dt.from_np(a.dtype), kind="ExternalInput").ap())
    args.append(nc.dram_tensor("out_dram", (B, T, D), _mybir.dt.float32, kind="ExternalOutput").ap())
    build(nc, *args)
    r = _run(nc, [arrays], core_ids=[0])
    return r.results[0]["out_dram"]
```

```python
import concourse.bass as bass
from concourse import mybir
from concourse.alu_op_type import AluOpType as ALU
from contextlib import ExitStack

F32 = mybir.dt.float32
F32R = mybir.dt.float32r
ACT = mybir.ActivationFunctionType
AX = mybir.AxisListType

B, T, D = 64, 128, 128
HID = 256
HALVES = HID // D
GATES = 4
I, F, G, O = range(GATES)
SKIPS = 4
NB = 4
COLS = NB * T
SLOTS = 2
CHUNKS = B // NB
EPS = 1e-5
FUNCS = {I: ACT.Sigmoid, F: ACT.Sigmoid, G: ACT.Tanh, O: ACT.Sigmoid}

ROW_BIH, ROW_BHH = 0, SKIPS * GATES
ROW_BG0 = 2 * SKIPS * GATES
ROW_B1 = ROW_BG0 + 1
ROW_G1 = ROW_B1 + HALVES
ROW_BE1 = ROW_G1 + HALVES
ROW_B2 = ROW_BE1 + HALVES
ROW_G2 = ROW_B2 + 1
ROW_BE2 = ROW_G2 + 1
NROWS = ROW_BE2 + 1


def lstm_plan(p):
    windows = T // p
    per_chunk = 8 if windows % 16 == 0 else 7
    return per_chunk, windows // (per_chunk * SLOTS)


def gates_of(step):
    return [I, G, O] if step == 0 else [I, G, F, O]


def need(engine, counter, value):
    if not (isinstance(value, int) and value <= 0):
        engine.wait_ge(counter, value)


def at_chunk(j, stage):
    c = j - stage
    return None if isinstance(c, int) and not 0 <= c < CHUNKS else c


def pipelined(engine, lag, unroll, iteration):
    first = -(-(lag + SLOTS) // unroll) * unroll
    for j in range(first):
        iteration(j, j % unroll)
    with engine.Fori(first, CHUNKS - unroll + 1, unroll) as j:
        for n in range(unroll):
            iteration(j + n, n)
    for j in range(CHUNKS, CHUNKS + lag):
        iteration(j, j % unroll)


def build(nc, x, adj, Wg0, bg0, Wg1, bg1, Wih, Whh, bih, bhh, W1, b1, g1, be1, W2, b2, g2, be2, out):
    x_v = x.rearrange("b t d -> t b d")
    out_v = out.rearrange("b t d -> t b d")
    kept = ExitStack()
    with kept:
        def sb(name, shape, dt=F32, where=kept):
            return where.enter_context(nc.sbuf_tensor(name, shape, dt))

        def sem(name):
            return kept.enter_context(nc.semaphore(name))

        H_hi = sb("H_hi", [128, T, B], F32R)
        H_lo = sb("H_lo", [128, T, B], F32R)
        ident = sb("ident", [128, 128])
        a_hatT = sb("a_hatT", [128, T])
        w1T = sb("w1T", [128, HALVES, D])
        w2T = sb("w2T", [128, HALVES, D])
        cols = sb("cols", [128, NROWS])
        gate_bias = sb("gate_bias", [128, SKIPS * GATES])
        bank = [kept.enter_context(nc.psum_tensor(f"bank{n}", [128, COLS], F32)) for n in range(8)]

        lstm_mem = ExitStack()
        w_hi = [[sb(f"w_hi{p}{k}", [128, GATES, D], F32R, lstm_mem) for k in range(1 if p == 0 else 2)] for p in range(SKIPS)]
        w_lo = [[sb(f"w_lo{p}{k}", [128, GATES, D], F32R, lstm_mem) for k in range(1 if p == 0 else 2)] for p in range(SKIPS)]

        gnn_mem = ExitStack()
        first_gnn(nc, sb, sem, gnn_mem, bank, x_v, adj, Wg0, bg0, Wg1, bg1, Wih, Whh, bih, bhh, W1, b1, g1, be1,
                  W2, b2, g2, be2, H_hi, H_lo, ident, a_hatT, w1T, w2T, cols, gate_bias, w_hi, w_lo)
        gnn_mem.close()
        lstms(nc, sb, sem, lstm_mem, bank, H_hi, H_lo, gate_bias, w_hi, w_lo)
        lstm_mem.close()
        second_gnn(nc, sb, sem, kept, bank, x_v, out_v, H_hi, H_lo, ident, a_hatT, w1T, w2T, cols)


def first_gnn(nc, sb, sem, mem, bank, x_v, adj, Wg0, bg0, Wg1, bg1, Wih, Whh, bih, bhh, W1, b1, g1, be1,
              W2, b2, g2, be2, H_hi, H_lo, ident, a_hatT, w1T, w2T, cols, gate_bias, w_hi, w_lo):
    AGG, H1, Z2, H2, CELL = 0, 1, 2, 3, 5
    P1_GATES = gates_of(0)
    NG = len(P1_GATES)

    def tile(name, shape, dt=F32):
        return sb(name, shape, dt, mem)

    adj_sb = tile("adj_sb", [128, T])
    adjT = tile("adjT", [128, T])
    a_norm = tile("a_norm", [128, T])
    a_normT = tile("a_normT", [128, T])
    a_diag = tile("a_diag", [128, T])
    a_half = tile("a_half", [128, T])
    degs = tile("degs", [128, 8])
    wg0 = tile("wg0", [128, D])
    wg1 = tile("wg1", [128, D])
    bg1_row = tile("bg1_row", [1, D])
    bg1_all = tile("bg1_all", [128, 1, D])
    ones = tile("ones", [128, 128])
    agg_bias = tile("agg_bias", [128, 1, T])
    rows = tile("rows", [NROWS, D])
    w1_nat = tile("w1_nat", [128, HALVES, D])
    w2_nat = tile("w2_nat", [128, HALVES, D])
    GROUPS = [(0, 0)] + [(p, k) for p in range(1, SKIPS) for k in range(2)]
    w_nat = [tile(f"w_nat{n}", [128, GATES, D]) for n in range(len(GROUPS))]
    xs = [tile(f"xs{k}", [128, NB, D]) for k in range(SLOTS)]
    agg = tile("agg", [128, COLS])
    pre1 = tile("pre1", [128, NB, T])
    h1 = tile("h1", [128, NB, T])
    z2 = tile("z2", [128, NB, D])
    h2_hi = [tile(f"h2_hi{k}", [128, COLS], F32R) for k in range(SLOTS)]
    h2_lo = [tile(f"h2_lo{k}", [128, COLS], F32R) for k in range(SLOTS)]
    gate = {g: tile(f"p1_gate{g}", [128, COLS]) for g in P1_GATES}
    cell = tile("p1_cell", [128, COLS])
    cell_tanh = tile("p1_cell_tanh", [128, COLS])
    state = tile("p1_state", [128, COLS])

    gate_bank = dict(zip(P1_GATES, bank))
    h2_bank, z2_bank, h1_bank, agg_bank, spare = bank[NG:NG + 5]

    adj_in, wg_in, small_in, rows_in = sem("adj_in"), sem("wg_in"), sem("small_in"), sem("rows_in")
    w_in = [sem(f"w_in{n}") for n in range(len(GROUPS))]
    ident_zero, ident_made = sem("ident_zero"), sem("ident_made")
    ones_made = sem("ones_made")
    prep_made = sem("prep_made")
    prep_hi = sem("prep_hi")
    prep_lo = sem("prep_lo")
    dve_prep = sem("dve_prep")
    act_prep = sem("act_prep")
    bias_made = sem("bias_made")
    root_out = sem("root_out")
    x_in = [sem(f"x_in{k}") for k in range(SLOTS)]
    agg_made, agg_out = sem("agg_made"), sem("agg_out")
    pre1_made, pre1_out = sem("pre1_made"), sem("pre1_out")
    h1_out = sem("h1_out")
    z2_made, z2_out = sem("z2_made"), sem("z2_out")
    h2_made, h2_hi_out, h2_lo_out = sem("h2_made"), sem("h2_hi_out"), sem("h2_lo_out")
    gates_made, gates_out = sem("p1_gates_made"), sem("p1_gates_out")
    cell_made, tanh_out = sem("p1_cell_made"), sem("p1_tanh_out")
    state_made, state_hi_out = sem("p1_state_made"), sem("p1_state_hi_out")

    P_ADJ, P_ROWS, P_W, P_HAT, P_LSTM = 1, 2, 3, 4, 5
    LATE = {CHUNKS + k: (1 + 2 * k, 2 + 2 * k) for k in range(len(GROUPS) // 2)}

    def group_bank(n):
        return agg_bank if n and n % 2 == 0 else spare

    def by_gate(ap):
        return ap.rearrange("p (g d) -> p g d", g=GATES)

    with nc.Block() as block:
        @block.sync
        def _(sp):
            sp.dma_start(adj_sb[:, :], adj).then_inc(adj_in, 16)
            for k in range(SLOTS):
                sp.dma_start(xs[k][:, :, :], x_v[:, k * NB:(k + 1) * NB, :]).then_inc(x_in[k], 16)
            sp.dma_start(wg0[:, :], Wg0).then_inc(wg_in, 16)
            sp.dma_start(wg1[:, :], Wg1).then_inc(wg_in, 16)
            sp.dma_start(bg1_row[:, :], bg1.rearrange("(o d) -> o d", o=1)).then_inc(wg_in, 16)
            sp.dma_start(w1_nat[:, :, :], W1.rearrange("(n h) d -> h n d", n=HALVES)).then_inc(small_in, 16)
            sp.dma_start(w2_nat[:, :, :], W2.rearrange("o (n h) -> o n h", n=HALVES)).then_inc(small_in, 16)
            with sp.Fori(SLOTS, CHUNKS - SLOTS + 1, SLOTS) as c:
                for k in range(SLOTS):
                    sp.wait_ge(agg_made, c + (k - SLOTS + 1))
                    sp.dma_start(xs[k][:, :, :], x_v[:, bass.ds((c + k) * NB, NB), :]).then_inc(x_in[k], 16)

        @block.gpsimd
        def _(pool):
            nc.gpsimd.memset(ident[:, :], 0.0).then_inc(ident_zero, 1)
            nc.gpsimd.memset(ones[:, :], 1.0).then_inc(ones_made, 1)
            pool.wait_ge(ident_zero, 1)
            nc.gpsimd.affine_select(out=ident[:, :], in_=ident[:, :], compare_op=ALU.not_equal, fill=1.0, base=0,
                                    pattern=[[-1, 128]], channel_multiplier=1).then_inc(ident_made, 1)

        @block.tensor
        def _(pe):
            def weight_group(n):
                pe.wait_ge(w_in[n], 16)
                need(pe, prep_lo, n - 1)
                for g in range(GATES):
                    last = nc.tensor.transpose(group_bank(n)[:, g * D:(g + 1) * D], w_nat[n][:, g, :], ident[:, :])
                last.then_inc(prep_made, 1)

            def early(j):
                if j == 0:
                    pe.wait_ge(rows_in, 16 * 9)
                    nc.tensor.transpose(bank[1][:, 0:NROWS], rows[:, :], ident[0:NROWS, 0:NROWS])
                    pe.wait_ge(act_prep, 1)
                    nc.tensor.matmul(bank[1][:, 128:256], ones[:, :], adjT[:, :], start=True, stop=True).then_inc(prep_made, 1)
                if j == 1:
                    pe.wait_ge(small_in, 32)
                    for n in range(HALVES):
                        nc.tensor.transpose(bank[2][:, n * D:(n + 1) * D], w1_nat[:, n, :], ident[:, :])
                    for n in range(HALVES):
                        last = nc.tensor.transpose(bank[2][:, (2 + n) * D:(3 + n) * D], w2_nat[:, n, :], ident[:, :])
                    last.then_inc(prep_made, 1)
                    pe.wait_ge(dve_prep, 7)
                    nc.tensor.transpose(bank[3][:, 0:T], a_half[:, :], ident[:, :]).then_inc(prep_made, 1)
                if j == 2:
                    weight_group(0)
                    pe.wait_ge(dve_prep, 9)
                    pe.wait_ge(act_prep, 3)

            pe.wait_ge(adj_in, 16)
            pe.wait_ge(ident_made, 1)
            nc.tensor.transpose(bank[0][:, 0:T], adj_sb[:, :], ident[:, :])
            pe.wait_ge(dve_prep, 1)
            nc.tensor.transpose(bank[0][:, 256:384], a_norm[:, :], ident[:, :])
            pe.wait_ge(wg_in, 48)
            pe.wait_ge(ones_made, 1)
            nc.tensor.matmul(bank[0][:, 128:256], ones[0:1, :], bg1_row[:, :], start=True, stop=True).then_inc(prep_made, 1)
            pe.wait_ge(act_prep, 1)

            def iteration(j, n):
                c, k = at_chunk(j, CELL), (n - CELL) % SLOTS
                if c is not None:
                    need(pe, gates_out, c * NG)
                    pe.wait_ge(h2_lo_out, c + 1)
                    for g in P1_GATES:
                        ps = gate_bank[g][:, :]
                        nc.tensor.matmul(ps, w_hi[0][0][:, g, :], h2_hi[k][:, :], start=True, stop=False)
                        nc.tensor.matmul(ps, w_hi[0][0][:, g, :], h2_lo[k][:, :], start=False, stop=False)
                        nc.tensor.matmul(ps, w_lo[0][0][:, g, :], h2_hi[k][:, :], start=False, stop=True).then_inc(gates_made, 1)
                c = at_chunk(j, H2)
                if c is not None:
                    pe.wait_ge(z2_out, c + 1)
                    for b in range(NB):
                        last = nc.tensor.matmul(h2_bank[:, b * T:(b + 1) * T], z2[:, b, :], adjT[:, :], start=True, stop=True)
                    last.then_inc(h2_made, 1)
                c = at_chunk(j, Z2)
                if c is not None:
                    pe.wait_ge(h1_out, c + 1)
                    for b in range(NB):
                        last = nc.tensor.matmul(z2_bank[:, b * D:(b + 1) * D], h1[:, b, :], wg1[:, :], start=True, stop=True)
                    last.then_inc(z2_made, 1)
                c = at_chunk(j, H1)
                if c is not None:
                    pe.wait_ge(agg_out, c + 1)
                    nc.tensor.matmul(h1_bank[:, :], wg0[:, :], agg[:, :], start=True, stop=True).then_inc(pre1_made, 1)
                c = at_chunk(j, AGG)
                if c is not None:
                    pe.wait_ge(x_in[n % SLOTS], (c - n % SLOTS) * (16 // SLOTS) + 16)
                    for b in range(NB):
                        last = nc.tensor.matmul(agg_bank[:, b * T:(b + 1) * T], xs[n % SLOTS][:, b, :], adjT[:, :], start=True, stop=True)
                    last.then_inc(agg_made, 1)
                if isinstance(j, int):
                    early(j)
                    for n in LATE.get(j, ()):
                        weight_group(n)

            pipelined(pe, CELL, SLOTS, iteration)

        @block.scalar
        def _(act):
            for n, (p, k) in enumerate(GROUPS):
                if n == 1:
                    act.dma_start(rows[ROW_BIH:ROW_BHH, :], bih.rearrange("p (g h) -> (p g) h", g=GATES)).then_inc(rows_in, 16)
                    act.dma_start(rows[ROW_BHH:ROW_BG0, :], bhh.rearrange("p (g h) -> (p g) h", g=GATES)).then_inc(rows_in, 16)
                    for row, v, size in ((ROW_BG0, bg0, 1), (ROW_B1, b1, HALVES), (ROW_G1, g1, HALVES), (ROW_BE1, be1, HALVES),
                                         (ROW_B2, b2, 1), (ROW_G2, g2, 1), (ROW_BE2, be2, 1)):
                        act.dma_start(rows[row:row + size, :], v.rearrange("(n h) -> n h", n=size)).then_inc(rows_in, 16)
                act.dma_start(w_nat[n][:, :, :], (Wih, Whh)[k][p].rearrange("(g h) d -> h g d", g=GATES)).then_inc(w_in[n], 16)

            def weight_group(n):
                p, k = GROUPS[n]
                act.wait_ge(prep_made, P_LSTM + n)
                nc.scalar.copy(w_hi[p][k][:, :, :], by_gate(group_bank(n)[:, :])).then_inc(prep_hi, 1)

            def early(j):
                if j == 0:
                    act.wait_ge(dve_prep, 5)
                    nc.scalar.activation(degs[:, 6:7], degs[:, 4:5], ACT.Sqrt).then_inc(root_out, 1)
                if j == 1:
                    act.wait_ge(prep_made, P_W)
                    nc.scalar.copy(w1T[:, :, :], bank[2][:, 0:2 * D].rearrange("p (n d) -> p n d", n=HALVES))
                    nc.scalar.copy(w2T[:, :, :], bank[2][:, 2 * D:4 * D].rearrange("p (n d) -> p n d", n=HALVES)).then_inc(act_prep, 1)
                if j == 2:
                    weight_group(0)

            act.wait_ge(prep_made, P_ADJ)
            nc.scalar.copy(adjT[:, :], bank[0][:, 0:T]).then_inc(act_prep, 1)
            nc.scalar.copy(bg1_all[:, 0, :], bank[0][:, 128:256])
            nc.scalar.copy(a_normT[:, :], bank[0][:, 256:384]).then_inc(act_prep, 1)

            def iteration(j, n):
                lstm = at_chunk(j, CELL)
                if lstm is not None:
                    need(act, state_made, lstm)
                    for k, g in enumerate(P1_GATES):
                        act.wait_ge(gates_made, lstm * NG + (k + 1))
                        nc.scalar.activation(gate[g][:, :], gate_bank[g][:, :], FUNCS[g],
                                             bias=gate_bias[:, g:g + 1]).then_inc(gates_out, 1)
                c, k = at_chunk(j, H2), (n - H2) % SLOTS
                if c is not None:
                    act.wait_ge(h2_made, c + 1)
                    nc.scalar.activation(h2_hi[k][:, :], h2_bank[:, :], ACT.Relu).then_inc(h2_hi_out, 1)
                if lstm is not None:
                    act.wait_ge(cell_made, lstm + 1)
                    nc.scalar.activation(cell_tanh[:, :], cell[:, :], ACT.Tanh).then_inc(tanh_out, 1)
                c = at_chunk(j, H1)
                if c is not None:
                    act.wait_ge(pre1_out, c + 1)
                    nc.scalar.activation(h1[:, :, :], pre1[:, :, :], ACT.Relu).then_inc(h1_out, 1)
                c = at_chunk(j, AGG)
                if c is not None:
                    act.wait_ge(agg_made, c + 1)
                    nc.scalar.copy(agg[:, :], agg_bank[:, :]).then_inc(agg_out, 1)
                if isinstance(j, int):
                    early(j)
                    for n in LATE.get(j, ()):
                        weight_group(n)

            pipelined(act, CELL, SLOTS, iteration)

        @block.vector
        def _(dve):
            done = [0]

            def step(ins):
                done[0] += 1
                ins.then_inc(dve_prep, 1)
                dve.wait_ge(dve_prep, done[0])

            def weight_group(n):
                p, k = GROUPS[n]
                dve.wait_ge(prep_hi, n + 1)
                nc.vector.tensor_tensor(w_lo[p][k][:, :, :], by_gate(group_bank(n)[:, :]), w_hi[p][k][:, :, :].bitcast(F32),
                                        ALU.subtract).then_inc(prep_lo, 1)

            def early(j):
                if j == 0:
                    dve.wait_ge(root_out, 1)
                    step(nc.vector.reciprocal(degs[:, 5:6], degs[:, 6:7]))
                    step(nc.vector.tensor_scalar(a_half[:, :], a_norm[:, :], degs[:, 5:6], None, ALU.mult))
                    dve.wait_ge(prep_made, P_ROWS)
                    step(nc.vector.tensor_copy(cols[:, :], bank[1][:, 0:NROWS]))
                    nc.vector.tensor_tensor(gate_bias[:, :], cols[:, ROW_BIH:ROW_BHH], cols[:, ROW_BHH:ROW_BG0], ALU.add)
                    nc.vector.tensor_scalar(agg_bias[:, 0, :], bank[1][:, 128:256], cols[:, ROW_BG0:ROW_BG0 + 1], None,
                                            ALU.mult).then_inc(bias_made, 1)
                    dve.wait_ge(bias_made, 1)
                if j == 1:
                    dve.wait_ge(prep_made, P_HAT)
                    step(nc.vector.tensor_scalar(a_hatT[:, :], bank[3][:, 0:T], degs[:, 5:6], None, ALU.mult))
                if j == 2:
                    weight_group(0)

            dve.wait_ge(adj_in, 16)
            dve.wait_ge(ident_made, 1)
            step(nc.vector.tensor_tensor(a_norm[:, :], adj_sb[:, :], ident[:, :], ALU.add))
            step(nc.vector.tensor_tensor(a_diag[:, :], a_norm[:, :], ident[:, :], ALU.mult))
            nc.vector.reduce_sum(degs[:, 0:1], a_norm[:, :], AX.X)
            nc.vector.reduce_sum(degs[:, 2:3], a_diag[:, :], AX.X)
            dve.wait_ge(act_prep, 2)
            step(nc.vector.reduce_sum(degs[:, 1:2], a_normT[:, :], AX.X))
            step(nc.vector.tensor_tensor(degs[:, 3:4], degs[:, 0:1], degs[:, 1:2], ALU.add))
            step(nc.vector.tensor_tensor(degs[:, 4:5], degs[:, 3:4], degs[:, 2:3], ALU.subtract))

            def iteration(j, n):
                lstm = at_chunk(j, CELL)
                if lstm is not None:
                    dve.wait_ge(gates_out, lstm * NG + 2)
                    nc.vector.tensor_tensor(cell[:, :], gate[I][:, :], gate[G][:, :], ALU.mult).then_inc(cell_made, 1)
                c, k = at_chunk(j, H2), (n - H2) % SLOTS
                if c is not None:
                    dve.wait_ge(h2_hi_out, c + 1)
                    nc.vector.scalar_tensor_tensor(out=h2_lo[k][:, :], in0=h2_bank[:, :], scalar=0.0, in1=h2_hi[k][:, :].bitcast(F32),
                                                   op0=ALU.max, op1=ALU.subtract).then_inc(h2_lo_out, 1)
                if lstm is not None:
                    dve.wait_ge(gates_out, lstm * NG + 3)
                    dve.wait_ge(tanh_out, lstm + 1)
                    nc.vector.tensor_tensor(state[:, :], gate[O][:, :], cell_tanh[:, :], ALU.mult).then_inc(state_made, 1)
                c = at_chunk(j, Z2)
                if c is not None:
                    dve.wait_ge(z2_made, c + 1)
                    nc.vector.tensor_tensor(z2[:, :, :], z2_bank[:, :].rearrange("p (b t) -> p b t", b=NB),
                                            bg1_all[:, :, :].to_broadcast([128, NB, D]), ALU.add).then_inc(z2_out, 1)
                c = at_chunk(j, H1)
                if c is not None:
                    dve.wait_ge(pre1_made, c + 1)
                    need(dve, h1_out, c)
                    nc.vector.tensor_tensor(pre1[:, :, :], h1_bank[:, :].rearrange("p (b t) -> p b t", b=NB),
                                            agg_bias[:, :, :].to_broadcast([128, NB, T]), ALU.add).then_inc(pre1_out, 1)
                if lstm is not None:
                    here = bass.ds(lstm * NB, NB)
                    by_time = state[:, :].rearrange("p (b t) -> p t b", b=NB)
                    dve.wait_ge(state_made, lstm + 1)
                    nc.vector.tensor_copy(H_hi[:, :, here], by_time).then_inc(state_hi_out, 1)
                    dve.wait_ge(state_hi_out, lstm + 1)
                    nc.vector.tensor_tensor(H_lo[:, :, here], by_time, H_hi[:, :, here].bitcast(F32), ALU.subtract)
                if isinstance(j, int):
                    early(j)
                    for n in LATE.get(j, ()):
                        weight_group(n)

            pipelined(dve, CELL, SLOTS, iteration)


def lstms(nc, sb, sem, mem, bank, H_hi, H_lo, gate_bias, w_hi, w_lo):
    act_sb = [[sb(f"gate{x}{g}", [128, COLS], F32, mem) for g in range(GATES)] for x in range(SLOTS)]
    cell = [sb(f"cell{x}", [128, COLS], F32, mem) for x in range(SLOTS)]
    cell_in = [sb(f"cell_in{x}", [128, COLS], F32, mem) for x in range(SLOTS)]
    cell_tanh = [sb(f"cell_tanh{x}", [128, COLS], F32, mem) for x in range(SLOTS)]
    state = [sb(f"state{x}", [128, COLS], F32, mem) for x in range(SLOTS)]
    state_hi = [sb(f"state_hi{x}", [128, COLS], F32R, mem) for x in range(SLOTS)]
    state_lo = [sb(f"state_lo{x}", [128, COLS], F32R, mem) for x in range(SLOTS)]

    gates_made = [sem(f"gates_made{x}") for x in range(SLOTS)]
    gates_out = [sem(f"gates_out{x}") for x in range(SLOTS)]
    cell_made = [sem(f"cell_made{x}") for x in range(SLOTS)]
    tanh_out = [sem(f"tanh_out{x}") for x in range(SLOTS)]
    state_out = [sem(f"state_out{x}") for x in range(SLOTS)]
    forgot = [sem(f"forgot{x}") for x in range(SLOTS)]
    split = [sem(f"split{x}") for x in range(SLOTS)]

    plan = []
    START = 2
    base = dict(gates=START, steps=START)
    for p in range(2, SKIPS + 1):
        per_chunk, iters = lstm_plan(p)
        per = dict(gates=len(gates_of(0)) + GATES * (p - 1), steps=p)
        plan.append((p, per_chunk, iters, dict(base), per))
        for key in base:
            base[key] += iters * per[key]

    def positions(buf, i, p, per_chunk, x, step):
        first = i * (SLOTS * per_chunk) + x * per_chunk
        grouped = buf[:, 0:T // p * p, :].rearrange("d (w s) b -> d w s b", s=p)
        return grouped[:, bass.ds(first, per_chunk), step, :]

    def earlier(i, p):
        covered, read = (SLOTS * lstm_plan(q)[0] * q for q in (p - 1, p))
        return i * (read // covered) + -(-read // covered)

    with nc.Block() as block:
        @block.gpsimd
        def _(pool):
            for counters in (gates_made, gates_out, cell_made, tanh_out, state_out, forgot, split):
                for x in range(SLOTS):
                    pool.sem_inc(counters[x], START)

        @block.tensor
        def _(pe):
            for p, per_chunk, iters, at, per in plan:
                n = per_chunk * B
                with pe.Fori(0, iters) as i:
                    if p > 2:
                        _, _, _, at0, per0 = plan[p - 3]
                        for y in range(SLOTS):
                            pe.wait_ge(state_out[y], earlier(i, p) * per0["steps"] + at0["steps"])
                    gate_no = 0
                    for step in range(p):
                        gates = gates_of(step)
                        for x in range(SLOTS):
                            pe.wait_ge(gates_out[x], i * per["gates"] + (at["gates"] + gate_no))
                            in_hi = positions(H_hi, i, p, per_chunk, x, step)
                            in_lo = positions(H_lo, i, p, per_chunk, x, step)
                            for g in gates:
                                ps = bank[x * GATES + g][:, 0:n]
                                nc.tensor.matmul(ps, w_hi[p - 1][0][:, g, :], in_hi, start=True, stop=False)
                                nc.tensor.matmul(ps, w_hi[p - 1][0][:, g, :], in_lo, start=False, stop=False)
                                last = nc.tensor.matmul(ps, w_lo[p - 1][0][:, g, :], in_hi, start=False, stop=step == 0)
                                if step == 0:
                                    last.then_inc(gates_made[x], 1)
                        if step > 0:
                            for x in range(SLOTS):
                                pe.wait_ge(state_out[x], i * per["steps"] + (at["steps"] + step))
                                for g in gates:
                                    ps = bank[x * GATES + g][:, 0:n]
                                    nc.tensor.matmul(ps, w_hi[p - 1][1][:, g, :], state_hi[x][:, 0:n], start=False, stop=False)
                                    nc.tensor.matmul(ps, w_hi[p - 1][1][:, g, :], state_lo[x][:, 0:n], start=False, stop=False)
                                    nc.tensor.matmul(ps, w_lo[p - 1][1][:, g, :], state_hi[x][:, 0:n],
                                                     start=False, stop=True).then_inc(gates_made[x], 1)
                        gate_no += len(gates)

        @block.scalar
        def _(act):
            for p, per_chunk, iters, at, per in plan:
                n = per_chunk * B

                def gate_functions(i, x, step, gate_no, which):
                    for k in which:
                        g, j = gates_of(step)[k], (p - 1) * GATES + gates_of(step)[k]
                        act.wait_ge(gates_made[x], i * per["gates"] + (at["gates"] + gate_no + k + 1))
                        nc.scalar.activation(act_sb[x][g][:, 0:n], bank[x * GATES + g][:, 0:n], FUNCS[g],
                                             bias=gate_bias[:, j:j + 1]).then_inc(gates_out[x], 1)

                def tanh_of_cell(i, x, step):
                    act.wait_ge(cell_made[x], i * per["steps"] + (at["steps"] + step + 1))
                    nc.scalar.activation(cell_tanh[x][:, 0:n], cell[x][:, 0:n], ACT.Tanh).then_inc(tanh_out[x], 1)

                with act.Fori(0, iters) as i:
                    gate_no = 0
                    for step in range(p):
                        count = len(gates_of(step))
                        for x in range(SLOTS):
                            if step == 0:
                                act.wait_ge(split[x], i * (2 * per["steps"]) + (2 * (at["steps"] - START) + START - 1))
                            gate_functions(i, x, step, gate_no, range(2))
                            if x > 0:
                                tanh_of_cell(i, x - 1, step)
                            gate_functions(i, x, step, gate_no, range(2, count))
                        tanh_of_cell(i, SLOTS - 1, step)
                        gate_no += count

        @block.vector
        def _(dve):
            base_forgot = START
            for p, per_chunk, iters, at, per in plan:
                n = per_chunk * B
                per_forgot = 2 * (p - 1)

                def cell_input(i, x, step, gate_no):
                    gate = act_sb[x]
                    dve.wait_ge(gates_out[x], i * per["gates"] + (at["gates"] + gate_no + 2))
                    target, counter = (cell[x], cell_made[x]) if step == 0 else (cell_in[x], forgot[x])
                    nc.vector.tensor_tensor(target[:, 0:n], gate[I][:, 0:n], gate[G][:, 0:n], ALU.mult).then_inc(counter, 1)

                def cell_update(i, x, step, gate_no):
                    gate = act_sb[x]
                    dve.wait_ge(gates_out[x], i * per["gates"] + (at["gates"] + gate_no + 3))
                    nc.vector.tensor_tensor(cell[x][:, 0:n], gate[F][:, 0:n], cell[x][:, 0:n], ALU.mult).then_inc(forgot[x], 1)
                    dve.wait_ge(forgot[x], i * per_forgot + (base_forgot + 2 * step))
                    nc.vector.tensor_tensor(cell[x][:, 0:n], cell[x][:, 0:n], cell_in[x][:, 0:n], ALU.add).then_inc(cell_made[x], 1)

                def new_state(i, x, step, gate_no):
                    dve.wait_ge(gates_out[x], i * per["gates"] + (at["gates"] + gate_no + len(gates_of(step))))
                    dve.wait_ge(tanh_out[x], i * per["steps"] + (at["steps"] + step + 1))
                    nc.vector.tensor_tensor(state[x][:, 0:n], act_sb[x][O][:, 0:n], cell_tanh[x][:, 0:n],
                                            ALU.mult).then_inc(split[x], 1)

                def split_state(i, x, step):
                    if step == p - 1:
                        to_hi = positions(H_hi, i, p, per_chunk, x, step)
                        to_lo = positions(H_lo, i, p, per_chunk, x, step)
                        st = state[x][:, 0:n].rearrange("p (w b) -> p w b", b=B)
                    else:
                        to_hi, to_lo, st = state_hi[x][:, 0:n], state_lo[x][:, 0:n], state[x][:, 0:n]
                    done = i * (2 * per["steps"]) + 2 * (at["steps"] - START + step) + START
                    dve.wait_ge(split[x], done + 1)
                    nc.vector.tensor_copy(to_hi, st).then_inc(split[x], 1)
                    dve.wait_ge(split[x], done + 2)
                    nc.vector.tensor_tensor(to_lo, st, to_hi.bitcast(F32), ALU.subtract).then_inc(state_out[x], 1)

                with dve.Fori(0, iters) as i:
                    gate_no = 0
                    for step in range(p):
                        for x in range(SLOTS):
                            cell_input(i, x, step, gate_no)
                            if x > 0:
                                new_state(i, x - 1, step, gate_no)
                            if step > 0:
                                cell_update(i, x, step, gate_no)
                            if x > 0:
                                split_state(i, x - 1, step)
                        new_state(i, SLOTS - 1, step, gate_no)
                        split_state(i, SLOTS - 1, step)
                        gate_no += len(gates_of(step))
                base_forgot += iters * per_forgot


def second_gnn(nc, sb, sem, mem, bank, x_v, out_v, H_hi, H_lo, ident, a_hatT, w1T, w2T, cols):
    x1 = sb("x1", [128, B, D])
    hid = [sb(f"hid{n}", [128, B * T]) for n in range(HALVES)]
    o_all = hid[0]
    RING = 4
    xr = [sb(f"xr{k}", [128, NB, D]) for k in range(SLOTS)]
    h_sum = [sb(f"h_sum{k}", [128, NB, T]) for k in range(SLOTS)]
    res = [sb(f"res{k}", [128, NB, D]) for k in range(SLOTS)]
    normed = [sb(f"normed{k}", [128, NB, D]) for k in range(RING)]
    hh = [sb(f"hh{k}", [128, HALVES, COLS]) for k in range(SLOTS)]
    agg = [hh[k][:, 0, :] for k in range(SLOTS)]
    y = h_sum
    st = [sb(f"st{k}", [128, NB, 6]) for k in range(SLOTS)]
    sums = [sb(f"sums{k}", [128, NB, 2]) for k in range(SLOTS)]
    diff, sqdiff, mean, var_sum, root, rstd, shift_row = (
        [sb(f"{n}{k}", [128, NB, 1]) for k in range(SLOTS)]
        for n in ("diff", "sqdiff", "mean", "var_sum", "root", "rstd", "shift_row"))
    eps = sb("eps", [128, 1])
    warm = sb("warm", [128, 1])
    bst = [sb(f"bst{n}", [128, CHUNKS, 6]) for n in range(3)]
    bmv = sb("bmv", [128, 3, 2])
    broot, brs, scale, mshift, shift = (sb(n, [128, 3, 1]) for n in ("broot", "brs", "scale", "mshift", "shift"))

    xr_in = [sem(f"xr_in{k}") for k in range(SLOTS)]
    stored = [sem(f"stored{k}") for k in range(RING)]
    eps_made, bn_root, bn_step, bn1_done, bn2_done = (sem(n) for n in ("eps_made", "bn_root", "bn_step", "bn1_done", "bn2_done"))
    hsum_out, hT_made, res_out = (sem(n) for n in ("hsum_out", "hT_made", "res_out"))
    x1_kept = [sem(f"x1_kept{k}") for k in range(SLOTS)]
    st_out, sums_out, sqdiff_out, var_out, root_out, rstd_out, shift_out, part_a, part_b = (
        sem(n) for n in ("st_out", "sums_out", "sqdiff_out", "var_out", "ln_root_out", "rstd_out", "shift_out", "part_a", "part_b"))
    agg_made, agg_out, hid_made, hid_out, bst_out = (sem(n) for n in ("agg2_made", "agg2_out", "hid_made", "hid_out", "bst_out"))
    hh_out, o_made, o_out, ost_out = (sem(n) for n in ("hh_out", "o_made", "o_out", "ost_out"))
    y_out, yT_made, res2_out = (sem(n) for n in ("y_out", "yT_made", "res2_out"))

    TURN, LN, LN_END, AGG, HIDDEN, STATS = range(6)

    def ln_start(dve, c, past, k):
        for b in range(NB):
            last = nc.vector.bn_stats(st[k][:, b, :], res[k][:, b, :])
        last.then_inc(st_out, 1)
        dve.wait_ge(st_out, c + (past + 1))
        nc.vector.tensor_tensor(sums[k][:, :, :], st[k][:, :, 1:3], st[k][:, :, 4:6], ALU.add)
        nc.vector.tensor_tensor(diff[k][:, :, 0], st[k][:, :, 1], st[k][:, :, 4], ALU.subtract).then_inc(sums_out, 1)
        dve.wait_ge(sums_out, c + (past + 1))
        nc.vector.tensor_scalar(mean[k][:, :, 0], sums[k][:, :, 0], 0.5, None, ALU.mult)
        nc.vector.scalar_tensor_tensor(out=sqdiff[k][:, :, 0], in0=diff[k][:, :, 0], scalar=D / 4, in1=diff[k][:, :, 0],
                                       op0=ALU.mult, op1=ALU.mult).then_inc(sqdiff_out, 1)
        dve.wait_ge(sqdiff_out, c + (past + 1))
        nc.vector.tensor_tensor(var_sum[k][:, :, 0], sqdiff[k][:, :, 0], sums[k][:, :, 1], ALU.add).then_inc(var_out, 1)

    def ln_root(act, c, past, k):
        act.wait_ge(var_out, c + (past + 1))
        nc.scalar.activation(root[k][:, :, 0], var_sum[k][:, :, 0], ACT.Sqrt, bias=eps[:, 0:1], scale=1.0 / D).then_inc(root_out, 1)

    def ln_scale(dve, c, past, k):
        dve.wait_ge(root_out, c + (past + 1))
        nc.vector.reciprocal(rstd[k][:, :, 0], root[k][:, :, 0]).then_inc(rstd_out, 1)
        dve.wait_ge(rstd_out, c + (past + 1))
        nc.vector.scalar_tensor_tensor(out=shift_row[k][:, :, 0], in0=mean[k][:, :, 0], scalar=-1.0, in1=rstd[k][:, :, 0],
                                       op0=ALU.mult, op1=ALU.mult).then_inc(shift_out, 1)

    def ln_by_act(act, c, past, k, target, batches):
        act.wait_ge(shift_out, c + (past + 1))
        for b in batches:
            last = nc.scalar.activation(target[:, b, :], res[k][:, b, :], ACT.Identity, bias=shift_row[k][:, b, :],
                                        scale=rstd[k][:, b, :])
        last.then_inc(part_a, 1)

    def ln_by_dve(k, target, batches):
        for b in batches:
            last = nc.vector.tensor_scalar(target[:, b, :], res[k][:, b, :], mean[k][:, b, 0:1], rstd[k][:, b, 0:1],
                                           ALU.subtract, ALU.mult)
        last.then_inc(part_b, 1)

    ACT1, DVE1 = range(0, 3), range(3, NB)
    ACT3, DVE3 = range(0, 3), range(3, NB)

    def batch_norm(dve, count, which, gain, bias, done):
        lo, hi = which[0], which[-1] + 1
        for n in which:
            last = nc.vector.bn_aggr(bmv[:, n, :], bst[n][:, :, :].rearrange("p c s -> p (c s)"))
        last.then_inc(bn_step, 1)
        dve.wait_ge(bn_root, count // 4 + 1)
        nc.vector.reciprocal(brs[:, lo:hi, 0], broot[:, lo:hi, 0]).then_inc(bn_step, 1)
        dve.wait_ge(bn_step, count + 2)
        nc.vector.tensor_tensor(scale[:, lo:hi, 0], brs[:, lo:hi, 0], gain, ALU.mult).then_inc(bn_step, 1)
        dve.wait_ge(bn_step, count + 3)
        nc.vector.tensor_tensor(mshift[:, lo:hi, 0], bmv[:, lo:hi, 0], scale[:, lo:hi, 0], ALU.mult).then_inc(bn_step, 1)
        dve.wait_ge(bn_step, count + 4)
        nc.vector.tensor_tensor(shift[:, lo:hi, 0], bias, mshift[:, lo:hi, 0], ALU.subtract).then_inc(done, 1)

    def columns(c):
        return bass.ds(c * COLS, COLS)

    def batches_of(c):
        return bass.ds(c * NB, NB)

    with nc.Block() as block:
        @block.sync
        def _(sp):
            def keep(c, k):
                sp.wait_ge(part_a, c + 1)
                sp.wait_ge(part_b, c + 1)
                sp.dma_start(x1[:, batches_of(c), :], normed[k][:, :, :]).then_inc(x1_kept[k], 16)

            for k in range(SLOTS):
                sp.dma_start(xr[k][:, :, :], x_v[:, k * NB:(k + 1) * NB, :]).then_inc(xr_in[k], 16)
            with sp.Fori(SLOTS, CHUNKS - SLOTS + 1, SLOTS) as c:
                for k in range(SLOTS):
                    sp.wait_ge(res_out, c + (k - SLOTS + 1))
                    sp.dma_start(xr[k][:, :, :], x_v[:, batches_of(c + k), :]).then_inc(xr_in[k], 16)
                    keep(c + (k - SLOTS), k)
            for c in range(CHUNKS - SLOTS, CHUNKS):
                keep(c, c % SLOTS)
            with sp.Fori(0, CHUNKS - RING + 1, RING) as c:
                for k in range(RING):
                    sp.wait_ge(part_a, c + (CHUNKS + k + 1))
                    sp.wait_ge(part_b, c + (CHUNKS + k + 1))
                    sp.dma_start(out_v[:, batches_of(c + k), :], normed[k][:, :, :]).then_inc(stored[k], 16)
            for k in range(RING):
                sp.wait_ge(stored[k], 16 * (CHUNKS // RING) + 16)

        @block.gpsimd
        def _(pool):
            for k in range(RING):
                pool.sem_inc(stored[k], 16)
            nc.gpsimd.memset(eps[:, :], EPS).then_inc(eps_made, 1)

            def sum_parts(c, n):
                k = n % SLOTS
                need(pool, hT_made, c + (1 - SLOTS))
                nc.gpsimd.tensor_tensor(h_sum[k][:, :, :].rearrange("p b t -> p t b"), H_hi[:, :, batches_of(c)].bitcast(F32),
                                        H_lo[:, :, batches_of(c)].bitcast(F32), ALU.add).then_inc(hsum_out, 1)

            pipelined(pool, 0, SLOTS, sum_parts)

        @block.tensor
        def _(pe):
            def first_pass(j, n):
                c, k = at_chunk(j, AGG), (n - AGG) % SLOTS
                if c is not None:
                    pe.wait_ge(part_a, c + 1)
                    pe.wait_ge(part_b, c + 1)
                    need(pe, agg_out, c + (1 - SLOTS))
                    for b in range(NB):
                        last = nc.tensor.matmul(bank[2 + k][:, b * T:(b + 1) * T], normed[k][:, b, :], a_hatT[:, :], start=True, stop=True)
                    last.then_inc(agg_made, 1)
                c, k = at_chunk(j, HIDDEN), (n - HIDDEN) % SLOTS
                if c is not None:
                    pe.wait_ge(agg_out, c + 1)
                    need(pe, hid_out, c + (1 - SLOTS))
                    for h in range(HALVES):
                        last = nc.tensor.matmul(bank[4 + 2 * k + h][:, :], w1T[:, h, :], agg[k], start=True, stop=True)
                    last.then_inc(hid_made, 1)
                c, k = at_chunk(j, TURN), (n - TURN) % SLOTS
                if c is not None:
                    pe.wait_ge(hsum_out, c + 1)
                    need(pe, res_out, c + (1 - SLOTS))
                    for b in range(NB):
                        last = nc.tensor.transpose(bank[k][:, b * D:(b + 1) * D], h_sum[k][:, b, :], ident[:, :])
                    last.then_inc(hT_made, 1)

            def second_pass(c, n):
                k = n % SLOTS
                pe.wait_ge(hh_out, c + 1)
                need(pe, o_out, c + (1 - SLOTS))
                for h in range(HALVES):
                    last = nc.tensor.matmul(bank[k][:, :], w2T[:, h, :], hh[k][:, h, :], start=h == 0, stop=h == HALVES - 1)
                last.then_inc(o_made, 1)

            def third_pass(c, n):
                k = n % SLOTS
                pe.wait_ge(y_out, c + 1)
                need(pe, res2_out, c + (1 - SLOTS))
                for b in range(NB):
                    last = nc.tensor.transpose(bank[2 + k][:, b * D:(b + 1) * D], y[k][:, b, :], ident[:, :])
                last.then_inc(yT_made, 1)

            pipelined(pe, HIDDEN, SLOTS, first_pass)
            pipelined(pe, 0, SLOTS, second_pass)
            pipelined(pe, 0, SLOTS, third_pass)

        @block.scalar
        def _(act):
            act.wait_ge(eps_made, 1)
            nc.scalar.activation(warm[:, :], eps[:, :], ACT.Sqrt)

            def first_pass(j, n):
                c, k = at_chunk(j, AGG), (n - AGG) % SLOTS
                if c is not None:
                    act.wait_ge(agg_made, c + 1)
                    nc.scalar.copy(agg[k], bank[2 + k][:, :]).then_inc(agg_out, 1)
                c, k = at_chunk(j, LN_END), (n - LN_END) % SLOTS
                if c is not None:
                    ln_by_act(act, c, 0, k, normed[k], ACT1)
                c, k = at_chunk(j, HIDDEN), (n - HIDDEN) % SLOTS
                if c is not None:
                    act.wait_ge(hid_made, c + 1)
                    for h in range(HALVES):
                        last = nc.scalar.activation(hid[h][:, columns(c)], bank[4 + 2 * k + h][:, :],
                                                    ACT.Identity, bias=cols[:, ROW_B1 + h:ROW_B1 + h + 1])
                    last.then_inc(hid_out, 1)
                c, k = at_chunk(j, LN), (n - LN) % SLOTS
                if c is not None:
                    ln_root(act, c, 0, k)

            def second_pass(c, n):
                k = n % SLOTS
                need(act, o_made, c + (1 - SLOTS))
                for h in range(HALVES):
                    last = nc.scalar.activation(hh[k][:, h, :], hid[h][:, columns(c)],
                                                ACT.Relu, bias=shift[:, h, :], scale=scale[:, h, :])
                last.then_inc(hh_out, 1)

            def third_pass(j, n):
                c, k = at_chunk(j, TURN), (n - TURN) % SLOTS
                if c is not None:
                    need(act, yT_made, c + (1 - SLOTS))
                    nc.scalar.activation(y[k][:, :, :].rearrange("p b t -> p (b t)"), o_all[:, columns(c)],
                                         ACT.Identity, bias=shift[:, 2, :], scale=scale[:, 2, :]).then_inc(y_out, 1)
                c, k, ring = at_chunk(j, LN_END), (n - LN_END) % SLOTS, (n - LN_END) % RING
                if c is not None:
                    ln_by_act(act, c, CHUNKS, k, normed[ring], ACT3)
                c, k = at_chunk(j, LN), (n - LN) % SLOTS
                if c is not None:
                    ln_root(act, c, CHUNKS, k)

            pipelined(act, HIDDEN, SLOTS, first_pass)
            act.wait_ge(bn_step, 1)
            nc.scalar.activation(broot[:, 0:2, 0], bmv[:, 0:2, 1], ACT.Sqrt, bias=eps[:, 0:1]).then_inc(bn_root, 1)
            act.wait_ge(bn1_done, 1)
            pipelined(act, 0, SLOTS, second_pass)
            act.wait_ge(bn_step, 5)
            nc.scalar.activation(broot[:, 2:3, 0], bmv[:, 2:3, 1], ACT.Sqrt, bias=eps[:, 0:1]).then_inc(bn_root, 1)
            act.wait_ge(bn2_done, 1)
            pipelined(act, LN_END, RING, third_pass)

        @block.vector
        def _(dve):
            def first_pass(j, n):
                c, k = at_chunk(j, LN), (n - LN) % SLOTS
                if c is not None:
                    dve.wait_ge(hT_made, c + 1)
                    dve.wait_ge(xr_in[k], (c - k) * (16 // SLOTS) + 16)
                    need(dve, part_a, c + (1 - SLOTS))
                    nc.vector.tensor_tensor(res[k][:, :, :], bank[k][:, :].rearrange("p (b d) -> p b d", b=NB),
                                            xr[k][:, :, :], ALU.add).then_inc(res_out, 1)
                c, k = at_chunk(j, LN_END), (n - LN_END) % SLOTS
                if c is not None:
                    need(dve, x1_kept[k], (c - k) * (16 // SLOTS))
                    need(dve, agg_made, c + (1 - SLOTS))
                    ln_scale(dve, c, 0, k)
                    ln_by_dve(k, normed[k], DVE1)
                c, k = at_chunk(j, LN), (n - LN) % SLOTS
                if c is not None:
                    dve.wait_ge(res_out, c + 1)
                    ln_start(dve, c, 0, k)
                c = at_chunk(j, STATS)
                if c is not None:
                    dve.wait_ge(hid_out, c + 1)
                    for h in range(HALVES):
                        last = nc.vector.bn_stats(bst[h][:, bass.ds(c, 1), :].rearrange("p c s -> p (c s)"), hid[h][:, columns(c)])
                    last.then_inc(bst_out, 1)

            def second_pass(c, n):
                k = n % SLOTS
                dve.wait_ge(o_made, c + 1)
                nc.vector.tensor_scalar(o_all[:, columns(c)], bank[k][:, :], cols[:, ROW_B2:ROW_B2 + 1], None, ALU.add).then_inc(o_out, 1)
                dve.wait_ge(o_out, c + 1)
                nc.vector.bn_stats(bst[2][:, bass.ds(c, 1), :].rearrange("p c s -> p (c s)"), o_all[:, columns(c)]).then_inc(ost_out, 1)

            def third_pass(j, n):
                c, k = at_chunk(j, LN), (n - LN) % SLOTS
                if c is not None:
                    dve.wait_ge(yT_made, c + 1)
                    need(dve, part_a, c + (CHUNKS + 1 - SLOTS))
                    nc.vector.tensor_tensor(res[k][:, :, :], bank[2 + k][:, :].rearrange("p (b d) -> p b d", b=NB),
                                            x1[:, batches_of(c), :], ALU.add).then_inc(res2_out, 1)
                c, k, ring = at_chunk(j, LN_END), (n - LN_END) % SLOTS, (n - LN_END) % RING
                if c is not None:
                    dve.wait_ge(stored[ring], (c - ring) * (16 // RING) + 16)
                    ln_scale(dve, c, CHUNKS, k)
                    ln_by_dve(k, normed[ring], DVE3)
                c, k = at_chunk(j, LN), (n - LN) % SLOTS
                if c is not None:
                    dve.wait_ge(res2_out, c + 1)
                    ln_start(dve, c, CHUNKS, k)

            pipelined(dve, STATS, SLOTS, first_pass)
            dve.wait_ge(bst_out, CHUNKS)
            batch_norm(dve, 0, [0, 1], cols[:, ROW_G1:ROW_G1 + 2], cols[:, ROW_BE1:ROW_BE1 + 2], bn1_done)
            pipelined(dve, 0, SLOTS, second_pass)
            dve.wait_ge(ost_out, CHUNKS)
            batch_norm(dve, 4, [2], cols[:, ROW_G2:ROW_G2 + 1], cols[:, ROW_BE2:ROW_BE2 + 1], bn2_done)
            for k in range(SLOTS):
                dve.wait_ge(x1_kept[k], 16 * (CHUNKS // SLOTS))
            pipelined(dve, LN_END, RING, third_pass)


_INS = ["x", "adj", "L0_gnn_Wg0", "L0_gnn_bg0", "L0_gnn_Wg1", "L0_gnn_bg1", "L0_gnn_Wih", "L0_gnn_Whh", "L0_gnn_bih",
        "L0_gnn_bhh", "L1_gnn_W1", "L1_gnn_b1", "L1_gnn_g1", "L1_gnn_be1", "L1_gnn_W2", "L1_gnn_b2", "L1_gnn_g2",
        "L1_gnn_be2"]


def kernel(**inputs):
    import numpy as _np
    import concourse.bacc as _bacc
    from concourse import mybir as _mybir
    from concourse.bass_utils import run_bass_kernel_spmd as _run

    nc = _bacc.Bacc("TRN2", target_bir_lowering=False, num_devices=1)
    arrays, args = {}, []
    for name in _INS:
        a = _np.ascontiguousarray(inputs[name])
        arrays[f"in_{name}_dram"] = a
        args.append(nc.dram_tensor(f"in_{name}_dram", a.shape, _mybir.dt.from_np(a.dtype), kind="ExternalInput").ap())
    args.append(nc.dram_tensor("out_dram", (B, T, D), _mybir.dt.float32, kind="ExternalOutput").ap())
    build(nc, *args)
    r = _run(nc, [arrays], core_ids=[0])
    return r.results[0]["out_dram"]
```

```python
import concourse.bass as bass
from concourse import mybir
from concourse.alu_op_type import AluOpType as ALU
from contextlib import ExitStack

F32 = mybir.dt.float32
F32R = mybir.dt.float32r
ACT = mybir.ActivationFunctionType
AX = mybir.AxisListType

B, T, D = 64, 128, 128
HID = 256
HALVES = HID // D
GATES = 4
I, F, G, O = range(GATES)
SKIPS = 4
NB = 4
COLS = NB * T
SLOTS = 2
CHUNKS = B // NB
EPS = 1e-5
FUNCS = {I: ACT.Sigmoid, F: ACT.Sigmoid, G: ACT.Tanh, O: ACT.Sigmoid}

ROW_BIH, ROW_BHH = 0, SKIPS * GATES
ROW_BG0 = 2 * SKIPS * GATES
ROW_B1 = ROW_BG0 + 1
ROW_G1 = ROW_B1 + HALVES
ROW_BE1 = ROW_G1 + HALVES
ROW_B2 = ROW_BE1 + HALVES
ROW_G2 = ROW_B2 + 1
ROW_BE2 = ROW_G2 + 1
NROWS = ROW_BE2 + 1


def lstm_plan(p):
    windows = T // p
    per_chunk = 8 if windows % 16 == 0 else 7
    return per_chunk, windows // (per_chunk * SLOTS)


def gates_of(step):
    return [I, G, O] if step == 0 else [I, G, F, O]


def need(engine, counter, value):
    if not (isinstance(value, int) and value <= 0):
        engine.wait_ge(counter, value)


def at_chunk(j, stage):
    c = j - stage
    return None if isinstance(c, int) and not 0 <= c < CHUNKS else c


def pipelined(engine, lag, unroll, iteration):
    first = -(-(lag + SLOTS) // unroll) * unroll
    for j in range(first):
        iteration(j, j % unroll)
    with engine.Fori(first, CHUNKS - unroll + 1, unroll) as j:
        for n in range(unroll):
            iteration(j + n, n)
    for j in range(CHUNKS, CHUNKS + lag):
        iteration(j, j % unroll)


def build(nc, x, adj, Wg0, bg0, Wg1, bg1, Wih, Whh, bih, bhh, W1, b1, g1, be1, W2, b2, g2, be2, out):
    x_v = x.rearrange("b t d -> t b d")
    out_v = out.rearrange("b t d -> t b d")
    kept = ExitStack()
    with kept:
        def sb(name, shape, dt=F32, where=kept):
            return where.enter_context(nc.sbuf_tensor(name, shape, dt))

        def sem(name):
            return kept.enter_context(nc.semaphore(name))

        H_hi = sb("H_hi", [128, T, B], F32R)
        H_lo = sb("H_lo", [128, T, B], F32R)
        ident = sb("ident", [128, 128])
        a_hatT = sb("a_hatT", [128, T])
        w1T = sb("w1T", [128, HALVES, D])
        w2T = sb("w2T", [128, HALVES, D])
        cols = sb("cols", [128, NROWS])
        gate_bias = sb("gate_bias", [128, SKIPS * GATES])
        bank = [kept.enter_context(nc.psum_tensor(f"bank{n}", [128, COLS], F32)) for n in range(8)]

        lstm_mem = ExitStack()
        w_hi = [[sb(f"w_hi{p}{k}", [128, GATES, D], F32R, lstm_mem) for k in range(1 if p == 0 else 2)] for p in range(SKIPS)]
        w_lo = [[sb(f"w_lo{p}{k}", [128, GATES, D], F32R, lstm_mem) for k in range(1 if p == 0 else 2)] for p in range(SKIPS)]

        gnn_mem = ExitStack()
        first_gnn(nc, sb, sem, gnn_mem, bank, x_v, adj, Wg0, bg0, Wg1, bg1, Wih, Whh, bih, bhh, W1, b1, g1, be1,
                  W2, b2, g2, be2, H_hi, H_lo, ident, a_hatT, w1T, w2T, cols, gate_bias, w_hi, w_lo)
        gnn_mem.close()
        lstms(nc, sb, sem, lstm_mem, bank, H_hi, H_lo, gate_bias, w_hi, w_lo)
        lstm_mem.close()
        second_gnn(nc, sb, sem, kept, bank, x_v, out_v, H_hi, H_lo, ident, a_hatT, w1T, w2T, cols)


def first_gnn(nc, sb, sem, mem, bank, x_v, adj, Wg0, bg0, Wg1, bg1, Wih, Whh, bih, bhh, W1, b1, g1, be1,
              W2, b2, g2, be2, H_hi, H_lo, ident, a_hatT, w1T, w2T, cols, gate_bias, w_hi, w_lo):
    AGG, H1, Z2, H2, CELL = 0, 1, 2, 3, 5
    P1_GATES = gates_of(0)
    NG = len(P1_GATES)

    def tile(name, shape, dt=F32):
        return sb(name, shape, dt, mem)

    adj_sb = tile("adj_sb", [128, T])
    adjT = tile("adjT", [128, T])
    a_norm = tile("a_norm", [128, T])
    a_normT = tile("a_normT", [128, T])
    a_diag = tile("a_diag", [128, T])
    a_half = tile("a_half", [128, T])
    degs = tile("degs", [128, 8])
    wg0 = tile("wg0", [128, D])
    wg1 = tile("wg1", [128, D])
    bg1_row = tile("bg1_row", [1, D])
    bg1_all = tile("bg1_all", [128, 1, D])
    ones = tile("ones", [128, 128])
    agg_bias = tile("agg_bias", [128, 1, T])
    rows = tile("rows", [NROWS, D])
    w1_nat = tile("w1_nat", [128, HALVES, D])
    w2_nat = tile("w2_nat", [128, HALVES, D])
    GROUPS = [(0, 0)] + [(p, k) for p in range(1, SKIPS) for k in range(2)]
    w_nat = [tile(f"w_nat{n}", [128, GATES, D]) for n in range(len(GROUPS))]
    xs = [tile(f"xs{k}", [128, NB, D]) for k in range(SLOTS)]
    agg = tile("agg", [128, COLS])
    pre1 = tile("pre1", [128, NB, T])
    h1 = tile("h1", [128, NB, T])
    z2 = tile("z2", [128, NB, D])
    h2_hi = [tile(f"h2_hi{k}", [128, COLS], F32R) for k in range(SLOTS)]
    h2_lo = [tile(f"h2_lo{k}", [128, COLS], F32R) for k in range(SLOTS)]
    gate = {g: tile(f"p1_gate{g}", [128, COLS]) for g in P1_GATES}
    cell = tile("p1_cell", [128, COLS])
    cell_tanh = tile("p1_cell_tanh", [128, COLS])
    state = tile("p1_state", [128, COLS])

    gate_bank = dict(zip(P1_GATES, bank))
    h2_bank, z2_bank, h1_bank, agg_bank, spare = bank[NG:NG + 5]

    adj_in, wg_in, small_in = sem("adj_in"), sem("wg_in"), sem("small_in")
    rows_by_act, rows_by_pool = sem("rows_by_act"), sem("rows_by_pool")
    w_in = [sem(f"w_in{n}") for n in range(len(GROUPS))]
    ident_zero, ident_made = sem("ident_zero"), sem("ident_made")
    ones_made = sem("ones_made")
    prep_made = sem("prep_made")
    prep_hi = sem("prep_hi")
    prep_lo = sem("prep_lo")
    dve_prep = sem("dve_prep")
    act_prep = sem("act_prep")
    bias_made = sem("bias_made")
    root_out = sem("root_out")
    x_in = [sem(f"x_in{k}") for k in range(SLOTS)]
    agg_made, agg_out = sem("agg_made"), sem("agg_out")
    pre1_made, pre1_out = sem("pre1_made"), sem("pre1_out")
    h1_out = sem("h1_out")
    z2_made, z2_out = sem("z2_made"), sem("z2_out")
    h2_made, h2_hi_out, h2_lo_out = sem("h2_made"), sem("h2_hi_out"), sem("h2_lo_out")
    gates_made, gates_out = sem("p1_gates_made"), sem("p1_gates_out")
    cell_made, tanh_out = sem("p1_cell_made"), sem("p1_tanh_out")
    state_made, state_hi_out = sem("p1_state_made"), sem("p1_state_hi_out")

    P_ADJ, P_ROWS, P_W, P_HAT, P_LSTM = 1, 2, 3, 4, 5
    LATE = {CHUNKS + k: (1 + 2 * k, 2 + 2 * k) for k in range(len(GROUPS) // 2)}

    def group_bank(n):
        return agg_bank if n and n % 2 == 0 else spare

    def by_gate(ap):
        return ap.rearrange("p (g d) -> p g d", g=GATES)

    def load_lstm_weights(engine, n):
        p, k = GROUPS[n]
        engine.dma_start(w_nat[n][:, :, :], (Wih, Whh)[k][p].rearrange("(g h) d -> h g d", g=GATES)).then_inc(w_in[n], 16)

    VECTORS = ((ROW_BIH, bih.rearrange("p (g h) -> (p g) h", g=GATES), SKIPS * GATES),
               (ROW_BHH, bhh.rearrange("p (g h) -> (p g) h", g=GATES), SKIPS * GATES),
               *((row, v.rearrange("(n h) -> n h", n=size), size) for row, v, size in (
                   (ROW_B1, b1, HALVES), (ROW_G1, g1, HALVES), (ROW_BE1, be1, HALVES), (ROW_BG0, bg0, 1),
                   (ROW_B2, b2, 1), (ROW_G2, g2, 1), (ROW_BE2, be2, 1))))
    VECTORS_BY_ACT = 4

    def load_vector(engine, n, counter):
        row, v, size = VECTORS[n]
        engine.dma_start(rows[row:row + size, :], v).then_inc(counter, 16)

    with nc.Block() as block:
        @block.sync
        def _(sp):
            def load_x(k):
                sp.dma_start(xs[k][:, :, :], x_v[:, k * NB:(k + 1) * NB, :]).then_inc(x_in[k], 16)

            sp.dma_start(adj_sb[:, :], adj).then_inc(adj_in, 16)
            load_x(0)
            sp.dma_start(bg1_row[:, :], bg1.rearrange("(o d) -> o d", o=1)).then_inc(wg_in, 16)
            sp.dma_start(wg0[:, :], Wg0).then_inc(wg_in, 16)
            sp.dma_start(wg1[:, :], Wg1).then_inc(wg_in, 16)
            load_x(1)
            load_lstm_weights(sp, 0)
            with sp.Fori(SLOTS, CHUNKS - SLOTS + 1, SLOTS) as c:
                for k in range(SLOTS):
                    sp.wait_ge(agg_made, c + (k - SLOTS + 1))
                    sp.dma_start(xs[k][:, :, :], x_v[:, bass.ds((c + k) * NB, NB), :]).then_inc(x_in[k], 16)

        @block.gpsimd
        def _(pool):
            nc.gpsimd.memset(ident[:, :], 0.0).then_inc(ident_zero, 1)
            nc.gpsimd.memset(ones[:, :], 1.0).then_inc(ones_made, 1)
            pool.wait_ge(ident_zero, 1)
            nc.gpsimd.affine_select(out=ident[:, :], in_=ident[:, :], compare_op=ALU.not_equal, fill=1.0, base=0,
                                    pattern=[[-1, 128]], channel_multiplier=1).then_inc(ident_made, 1)
            for n in range(VECTORS_BY_ACT, len(VECTORS)):
                load_vector(pool, n, rows_by_pool)
            pool.dma_start(w1_nat[:, :, :], W1.rearrange("(n h) d -> h n d", n=HALVES)).then_inc(small_in, 16)
            pool.dma_start(w2_nat[:, :, :], W2.rearrange("o (n h) -> o n h", n=HALVES)).then_inc(small_in, 16)
            for n in range(1, len(GROUPS)):
                load_lstm_weights(pool, n)

        @block.tensor
        def _(pe):
            def weight_group(n):
                pe.wait_ge(w_in[n], 16)
                need(pe, prep_lo, n - 1)
                for g in range(GATES):
                    last = nc.tensor.transpose(group_bank(n)[:, g * D:(g + 1) * D], w_nat[n][:, g, :], ident[:, :])
                last.then_inc(prep_made, 1)

            def early(j):
                if j == 0:
                    pe.wait_ge(rows_by_act, 16 * VECTORS_BY_ACT)
                    pe.wait_ge(rows_by_pool, 16 * (len(VECTORS) - VECTORS_BY_ACT))
                    nc.tensor.transpose(bank[1][:, 0:NROWS], rows[:, :], ident[0:NROWS, 0:NROWS])
                    pe.wait_ge(act_prep, 1)
                    nc.tensor.matmul(bank[1][:, 128:256], ones[:, :], adjT[:, :], start=True, stop=True).then_inc(prep_made, 1)
                if j == 1:
                    pe.wait_ge(small_in, 32)
                    for n in range(HALVES):
                        nc.tensor.transpose(bank[2][:, n * D:(n + 1) * D], w1_nat[:, n, :], ident[:, :])
                    for n in range(HALVES):
                        last = nc.tensor.transpose(bank[2][:, (2 + n) * D:(3 + n) * D], w2_nat[:, n, :], ident[:, :])
                    last.then_inc(prep_made, 1)
                    pe.wait_ge(dve_prep, 7)
                    nc.tensor.transpose(bank[3][:, 0:T], a_half[:, :], ident[:, :]).then_inc(prep_made, 1)
                if j == 2:
                    weight_group(0)
                    pe.wait_ge(dve_prep, 9)
                    pe.wait_ge(act_prep, 3)

            pe.wait_ge(adj_in, 16)
            pe.wait_ge(ident_made, 1)
            nc.tensor.transpose(bank[0][:, 0:T], adj_sb[:, :], ident[:, :])
            pe.wait_ge(dve_prep, 1)
            nc.tensor.transpose(bank[0][:, 256:384], a_norm[:, :], ident[:, :])
            pe.wait_ge(wg_in, 48)
            pe.wait_ge(ones_made, 1)
            nc.tensor.matmul(bank[0][:, 128:256], ones[0:1, :], bg1_row[:, :], start=True, stop=True).then_inc(prep_made, 1)
            pe.wait_ge(act_prep, 1)

            def iteration(j, n):
                c, k = at_chunk(j, CELL), (n - CELL) % SLOTS
                if c is not None:
                    need(pe, gates_out, c * NG)
                    pe.wait_ge(h2_lo_out, c + 1)
                    for g in P1_GATES:
                        ps = gate_bank[g][:, :]
                        nc.tensor.matmul(ps, w_hi[0][0][:, g, :], h2_hi[k][:, :], start=True, stop=False)
                        nc.tensor.matmul(ps, w_hi[0][0][:, g, :], h2_lo[k][:, :], start=False, stop=False)
                        nc.tensor.matmul(ps, w_lo[0][0][:, g, :], h2_hi[k][:, :], start=False, stop=True).then_inc(gates_made, 1)
                c = at_chunk(j, H2)
                if c is not None:
                    pe.wait_ge(z2_out, c + 1)
                    need(pe, h2_lo_out, c)
                    for b in range(NB):
                        last = nc.tensor.matmul(h2_bank[:, b * T:(b + 1) * T], z2[:, b, :], adjT[:, :], start=True, stop=True)
                    last.then_inc(h2_made, 1)
                c = at_chunk(j, Z2)
                if c is not None:
                    pe.wait_ge(h1_out, c + 1)
                    for b in range(NB):
                        last = nc.tensor.matmul(z2_bank[:, b * D:(b + 1) * D], h1[:, b, :], wg1[:, :], start=True, stop=True)
                    last.then_inc(z2_made, 1)
                c = at_chunk(j, H1)
                if c is not None:
                    pe.wait_ge(agg_out, c + 1)
                    nc.tensor.matmul(h1_bank[:, :], wg0[:, :], agg[:, :], start=True, stop=True).then_inc(pre1_made, 1)
                c = at_chunk(j, AGG)
                if c is not None:
                    pe.wait_ge(x_in[n % SLOTS], (c - n % SLOTS) * (16 // SLOTS) + 16)
                    for b in range(NB):
                        last = nc.tensor.matmul(agg_bank[:, b * T:(b + 1) * T], xs[n % SLOTS][:, b, :], adjT[:, :], start=True, stop=True)
                    last.then_inc(agg_made, 1)
                if isinstance(j, int):
                    early(j)
                    for n in LATE.get(j, ()):
                        weight_group(n)

            pipelined(pe, CELL, SLOTS, iteration)

        @block.scalar
        def _(act):
            for n in range(VECTORS_BY_ACT):
                load_vector(act, n, rows_by_act)

            def weight_group(n):
                p, k = GROUPS[n]
                act.wait_ge(prep_made, P_LSTM + n)
                nc.scalar.copy(w_hi[p][k][:, :, :], by_gate(group_bank(n)[:, :])).then_inc(prep_hi, 1)

            def early(j):
                if j == 0:
                    act.wait_ge(dve_prep, 5)
                    nc.scalar.activation(degs[:, 6:7], degs[:, 4:5], ACT.Sqrt).then_inc(root_out, 1)
                if j == 1:
                    act.wait_ge(prep_made, P_W)
                    nc.scalar.copy(w1T[:, :, :], bank[2][:, 0:2 * D].rearrange("p (n d) -> p n d", n=HALVES))
                    nc.scalar.copy(w2T[:, :, :], bank[2][:, 2 * D:4 * D].rearrange("p (n d) -> p n d", n=HALVES)).then_inc(act_prep, 1)
                if j == 2:
                    weight_group(0)

            act.wait_ge(prep_made, P_ADJ)
            nc.scalar.copy(adjT[:, :], bank[0][:, 0:T]).then_inc(act_prep, 1)
            nc.scalar.copy(bg1_all[:, 0, :], bank[0][:, 128:256])
            nc.scalar.copy(a_normT[:, :], bank[0][:, 256:384]).then_inc(act_prep, 1)

            def iteration(j, n):
                lstm = at_chunk(j, CELL)
                if lstm is not None:
                    need(act, state_made, lstm)
                    for k, g in enumerate(P1_GATES):
                        act.wait_ge(gates_made, lstm * NG + (k + 1))
                        nc.scalar.activation(gate[g][:, :], gate_bank[g][:, :], FUNCS[g],
                                             bias=gate_bias[:, g:g + 1]).then_inc(gates_out, 1)
                c, k = at_chunk(j, H2), (n - H2) % SLOTS
                if c is not None:
                    act.wait_ge(h2_made, c + 1)
                    nc.scalar.activation(h2_hi[k][:, :], h2_bank[:, :], ACT.Relu).then_inc(h2_hi_out, 1)
                c = at_chunk(j, H1)
                if c is not None:
                    act.wait_ge(pre1_out, c + 1)
                    nc.scalar.activation(h1[:, :, :], pre1[:, :, :], ACT.Relu).then_inc(h1_out, 1)
                if lstm is not None:
                    act.wait_ge(cell_made, lstm + 1)
                    nc.scalar.activation(cell_tanh[:, :], cell[:, :], ACT.Tanh).then_inc(tanh_out, 1)
                c = at_chunk(j, AGG)
                if c is not None:
                    act.wait_ge(agg_made, c + 1)
                    nc.scalar.copy(agg[:, :], agg_bank[:, :]).then_inc(agg_out, 1)
                if isinstance(j, int):
                    early(j)
                    for n in LATE.get(j, ()):
                        weight_group(n)

            pipelined(act, CELL, SLOTS, iteration)

        @block.vector
        def _(dve):
            done = [0]

            def step(ins):
                done[0] += 1
                ins.then_inc(dve_prep, 1)
                dve.wait_ge(dve_prep, done[0])

            def weight_group(n):
                p, k = GROUPS[n]
                dve.wait_ge(prep_hi, n + 1)
                nc.vector.tensor_tensor(w_lo[p][k][:, :, :], by_gate(group_bank(n)[:, :]), w_hi[p][k][:, :, :].bitcast(F32),
                                        ALU.subtract).then_inc(prep_lo, 1)

            def early(j):
                if j == 0:
                    dve.wait_ge(root_out, 1)
                    step(nc.vector.reciprocal(degs[:, 5:6], degs[:, 6:7]))
                    step(nc.vector.tensor_scalar(a_half[:, :], a_norm[:, :], degs[:, 5:6], None, ALU.mult))
                    dve.wait_ge(prep_made, P_ROWS)
                    step(nc.vector.tensor_copy(cols[:, :], bank[1][:, 0:NROWS]))
                    nc.vector.tensor_tensor(gate_bias[:, :], cols[:, ROW_BIH:ROW_BHH], cols[:, ROW_BHH:ROW_BG0], ALU.add)
                    nc.vector.tensor_scalar(agg_bias[:, 0, :], bank[1][:, 128:256], cols[:, ROW_BG0:ROW_BG0 + 1], None,
                                            ALU.mult).then_inc(bias_made, 1)
                    dve.wait_ge(bias_made, 1)
                if j == 1:
                    dve.wait_ge(prep_made, P_HAT)
                    step(nc.vector.tensor_scalar(a_hatT[:, :], bank[3][:, 0:T], degs[:, 5:6], None, ALU.mult))
                if j == 2:
                    weight_group(0)

            dve.wait_ge(adj_in, 16)
            dve.wait_ge(ident_made, 1)
            step(nc.vector.tensor_tensor(a_norm[:, :], adj_sb[:, :], ident[:, :], ALU.add))
            step(nc.vector.tensor_tensor(a_diag[:, :], a_norm[:, :], ident[:, :], ALU.mult))
            nc.vector.reduce_sum(degs[:, 0:1], a_norm[:, :], AX.X)
            nc.vector.reduce_sum(degs[:, 2:3], a_diag[:, :], AX.X)
            dve.wait_ge(act_prep, 2)
            step(nc.vector.reduce_sum(degs[:, 1:2], a_normT[:, :], AX.X))
            step(nc.vector.tensor_tensor(degs[:, 3:4], degs[:, 0:1], degs[:, 1:2], ALU.add))
            step(nc.vector.tensor_tensor(degs[:, 4:5], degs[:, 3:4], degs[:, 2:3], ALU.subtract))

            def iteration(j, n):
                lstm = at_chunk(j, CELL)
                if lstm is not None:
                    dve.wait_ge(gates_out, lstm * NG + 2)
                    nc.vector.tensor_tensor(cell[:, :], gate[I][:, :], gate[G][:, :], ALU.mult).then_inc(cell_made, 1)
                c = at_chunk(j, H1)
                if c is not None:
                    dve.wait_ge(pre1_made, c + 1)
                    need(dve, h1_out, c)
                    nc.vector.tensor_tensor(pre1[:, :, :], h1_bank[:, :].rearrange("p (b t) -> p b t", b=NB),
                                            agg_bias[:, :, :].to_broadcast([128, NB, T]), ALU.add).then_inc(pre1_out, 1)
                c = at_chunk(j, Z2)
                if c is not None:
                    dve.wait_ge(z2_made, c + 1)
                    nc.vector.tensor_tensor(z2[:, :, :], z2_bank[:, :].rearrange("p (b t) -> p b t", b=NB),
                                            bg1_all[:, :, :].to_broadcast([128, NB, D]), ALU.add).then_inc(z2_out, 1)
                c, k = at_chunk(j, H2), (n - H2) % SLOTS
                if c is not None:
                    dve.wait_ge(h2_hi_out, c + 1)
                    nc.vector.scalar_tensor_tensor(out=h2_lo[k][:, :], in0=h2_bank[:, :], scalar=0.0, in1=h2_hi[k][:, :].bitcast(F32),
                                                   op0=ALU.max, op1=ALU.subtract).then_inc(h2_lo_out, 1)
                if lstm is not None:
                    dve.wait_ge(gates_out, lstm * NG + 3)
                    dve.wait_ge(tanh_out, lstm + 1)
                    nc.vector.tensor_tensor(state[:, :], gate[O][:, :], cell_tanh[:, :], ALU.mult).then_inc(state_made, 1)
                if lstm is not None:
                    here = bass.ds(lstm * NB, NB)
                    by_time = state[:, :].rearrange("p (b t) -> p t b", b=NB)
                    dve.wait_ge(state_made, lstm + 1)
                    nc.vector.tensor_copy(H_hi[:, :, here], by_time).then_inc(state_hi_out, 1)
                    dve.wait_ge(state_hi_out, lstm + 1)
                    nc.vector.tensor_tensor(H_lo[:, :, here], by_time, H_hi[:, :, here].bitcast(F32), ALU.subtract)
                if isinstance(j, int):
                    early(j)
                    for n in LATE.get(j, ()):
                        weight_group(n)

            pipelined(dve, CELL, SLOTS, iteration)


def lstms(nc, sb, sem, mem, bank, H_hi, H_lo, gate_bias, w_hi, w_lo):
    act_sb = [[sb(f"gate{x}{g}", [128, COLS], F32, mem) for g in range(GATES)] for x in range(SLOTS)]
    cell = [sb(f"cell{x}", [128, COLS], F32, mem) for x in range(SLOTS)]
    cell_in = [sb(f"cell_in{x}", [128, COLS], F32, mem) for x in range(SLOTS)]
    cell_tanh = [sb(f"cell_tanh{x}", [128, COLS], F32, mem) for x in range(SLOTS)]
    state = [sb(f"state{x}", [128, COLS], F32, mem) for x in range(SLOTS)]
    state_hi = [sb(f"state_hi{x}", [128, COLS], F32R, mem) for x in range(SLOTS)]
    state_lo = [sb(f"state_lo{x}", [128, COLS], F32R, mem) for x in range(SLOTS)]

    gates_made = [sem(f"gates_made{x}") for x in range(SLOTS)]
    gates_out = [sem(f"gates_out{x}") for x in range(SLOTS)]
    cell_made = [sem(f"cell_made{x}") for x in range(SLOTS)]
    tanh_out = [sem(f"tanh_out{x}") for x in range(SLOTS)]
    state_out = [sem(f"state_out{x}") for x in range(SLOTS)]
    forgot = [sem(f"forgot{x}") for x in range(SLOTS)]
    split = [sem(f"split{x}") for x in range(SLOTS)]

    plan = []
    START = GATES
    base = dict(gates=START, steps=START)
    for p in range(2, SKIPS + 1):
        per_chunk, iters = lstm_plan(p)
        per = dict(gates=len(gates_of(0)) + GATES * (p - 1), steps=p)
        plan.append((p, per_chunk, iters, dict(base), per))
        for key in base:
            base[key] += iters * per[key]

    def positions(buf, i, p, per_chunk, x, step):
        first = i * (SLOTS * per_chunk) + x * per_chunk
        grouped = buf[:, 0:T // p * p, :].rearrange("d (w s) b -> d w s b", s=p)
        return grouped[:, bass.ds(first, per_chunk), step, :]

    def earlier(i, p):
        covered, read = (SLOTS * lstm_plan(q)[0] * q for q in (p - 1, p))
        return i * (read // covered) + -(-read // covered)

    with nc.Block() as block:
        @block.gpsimd
        def _(pool):
            for counters in (gates_made, gates_out, cell_made, tanh_out, state_out, forgot, split):
                for x in range(SLOTS):
                    pool.sem_inc(counters[x], START)

        @block.tensor
        def _(pe):
            for p, per_chunk, iters, at, per in plan:
                n = per_chunk * B
                with pe.Fori(0, iters) as i:
                    if p > 2:
                        _, _, _, at0, per0 = plan[p - 3]
                        for y in range(SLOTS):
                            pe.wait_ge(state_out[y], earlier(i, p) * per0["steps"] + at0["steps"])
                    gate_no = 0
                    for step in range(p):
                        gates = gates_of(step)
                        before = gates_of(step - 1 if step > 0 else p - 1)
                        for x in range(SLOTS):
                            in_hi = positions(H_hi, i, p, per_chunk, x, step)
                            in_lo = positions(H_lo, i, p, per_chunk, x, step)
                            for g in gates:
                                ps = bank[x * GATES + g][:, 0:n]
                                if g in before:
                                    pe.wait_ge(gates_out[x], i * per["gates"] + (
                                        at["gates"] + gate_no - len(before) + before.index(g) + 1))
                                nc.tensor.matmul(ps, w_hi[p - 1][0][:, g, :], in_hi, start=True, stop=False)
                                nc.tensor.matmul(ps, w_hi[p - 1][0][:, g, :], in_lo, start=False, stop=False)
                                last = nc.tensor.matmul(ps, w_lo[p - 1][0][:, g, :], in_hi, start=False, stop=step == 0)
                                if step == 0:
                                    last.then_inc(gates_made[x], 1)
                        if step > 0:
                            for x in range(SLOTS):
                                pe.wait_ge(state_out[x], i * per["steps"] + (at["steps"] + step))
                                for g in gates:
                                    ps = bank[x * GATES + g][:, 0:n]
                                    nc.tensor.matmul(ps, w_hi[p - 1][1][:, g, :], state_hi[x][:, 0:n], start=False, stop=False)
                                    nc.tensor.matmul(ps, w_hi[p - 1][1][:, g, :], state_lo[x][:, 0:n], start=False, stop=False)
                                    nc.tensor.matmul(ps, w_lo[p - 1][1][:, g, :], state_hi[x][:, 0:n],
                                                     start=False, stop=True).then_inc(gates_made[x], 1)
                        gate_no += len(gates)

        @block.scalar
        def _(act):
            for p, per_chunk, iters, at, per in plan:
                n = per_chunk * B

                def gate_functions(i, x, step, gate_no, which):
                    for k in which:
                        g, j = gates_of(step)[k], (p - 1) * GATES + gates_of(step)[k]
                        act.wait_ge(gates_made[x], i * per["gates"] + (at["gates"] + gate_no + k + 1))
                        nc.scalar.activation(act_sb[x][g][:, 0:n], bank[x * GATES + g][:, 0:n], FUNCS[g],
                                             bias=gate_bias[:, j:j + 1]).then_inc(gates_out[x], 1)

                def tanh_of_cell(i, x, step):
                    act.wait_ge(cell_made[x], i * per["steps"] + (at["steps"] + step + 1))
                    nc.scalar.activation(cell_tanh[x][:, 0:n], cell[x][:, 0:n], ACT.Tanh).then_inc(tanh_out[x], 1)

                with act.Fori(0, iters) as i:
                    gate_no = 0
                    for step in range(p):
                        count = len(gates_of(step))
                        for x in range(SLOTS):
                            if step == 0:
                                act.wait_ge(split[x], i * (2 * per["steps"]) + (2 * (at["steps"] - START) + START - 1))
                            gate_functions(i, x, step, gate_no, range(2))
                            if x > 0:
                                tanh_of_cell(i, x - 1, step)
                            gate_functions(i, x, step, gate_no, range(2, count))
                        tanh_of_cell(i, SLOTS - 1, step)
                        gate_no += count

        @block.vector
        def _(dve):
            base_forgot = START
            for p, per_chunk, iters, at, per in plan:
                n = per_chunk * B
                per_forgot = 2 * (p - 1)

                def cell_input(i, x, step, gate_no):
                    gate = act_sb[x]
                    dve.wait_ge(gates_out[x], i * per["gates"] + (at["gates"] + gate_no + 2))
                    target, counter = (cell[x], cell_made[x]) if step == 0 else (cell_in[x], forgot[x])
                    nc.vector.tensor_tensor(target[:, 0:n], gate[I][:, 0:n], gate[G][:, 0:n], ALU.mult).then_inc(counter, 1)

                def cell_update(i, x, step, gate_no):
                    gate = act_sb[x]
                    dve.wait_ge(gates_out[x], i * per["gates"] + (at["gates"] + gate_no + 3))
                    nc.vector.tensor_tensor(cell[x][:, 0:n], gate[F][:, 0:n], cell[x][:, 0:n], ALU.mult).then_inc(forgot[x], 1)
                    dve.wait_ge(forgot[x], i * per_forgot + (base_forgot + 2 * step))
                    nc.vector.tensor_tensor(cell[x][:, 0:n], cell[x][:, 0:n], cell_in[x][:, 0:n], ALU.add).then_inc(cell_made[x], 1)

                def new_state(i, x, step, gate_no):
                    dve.wait_ge(gates_out[x], i * per["gates"] + (at["gates"] + gate_no + len(gates_of(step))))
                    dve.wait_ge(tanh_out[x], i * per["steps"] + (at["steps"] + step + 1))
                    nc.vector.tensor_tensor(state[x][:, 0:n], act_sb[x][O][:, 0:n], cell_tanh[x][:, 0:n],
                                            ALU.mult).then_inc(split[x], 1)

                def split_state(i, x, step):
                    if step == p - 1:
                        to_hi = positions(H_hi, i, p, per_chunk, x, step)
                        to_lo = positions(H_lo, i, p, per_chunk, x, step)
                        st = state[x][:, 0:n].rearrange("p (w b) -> p w b", b=B)
                    else:
                        to_hi, to_lo, st = state_hi[x][:, 0:n], state_lo[x][:, 0:n], state[x][:, 0:n]
                    done = i * (2 * per["steps"]) + 2 * (at["steps"] - START + step) + START
                    dve.wait_ge(split[x], done + 1)
                    nc.vector.tensor_copy(to_hi, st).then_inc(split[x], 1)
                    dve.wait_ge(split[x], done + 2)
                    nc.vector.tensor_tensor(to_lo, st, to_hi.bitcast(F32), ALU.subtract).then_inc(state_out[x], 1)

                with dve.Fori(0, iters) as i:
                    gate_no = 0
                    for step in range(p):
                        for x in range(SLOTS):
                            cell_input(i, x, step, gate_no)
                            if x > 0:
                                new_state(i, x - 1, step, gate_no)
                            if step > 0:
                                cell_update(i, x, step, gate_no)
                            if x > 0:
                                split_state(i, x - 1, step)
                        new_state(i, SLOTS - 1, step, gate_no)
                        split_state(i, SLOTS - 1, step)
                        gate_no += len(gates_of(step))
                base_forgot += iters * per_forgot


def second_gnn(nc, sb, sem, mem, bank, x_v, out_v, H_hi, H_lo, ident, a_hatT, w1T, w2T, cols):
    x1 = sb("x1", [128, B, D])
    hid = [sb(f"hid{n}", [128, B * T]) for n in range(HALVES)]
    o_all = hid[0]
    RING = 4
    xr = [sb(f"xr{k}", [128, NB, D]) for k in range(SLOTS)]
    h_sum = [sb(f"h_sum{k}", [128, NB, T]) for k in range(SLOTS)]
    res = [sb(f"res{k}", [128, NB, D]) for k in range(SLOTS)]
    normed = [sb(f"normed{k}", [128, NB, D]) for k in range(RING)]
    hh = [sb(f"hh{k}", [128, HALVES, COLS]) for k in range(SLOTS)]
    agg = [hh[k][:, 0, :] for k in range(SLOTS)]
    x1_plus = h_sum
    st = [sb(f"st{k}", [128, NB, 6]) for k in range(RING)]
    sums = [sb(f"sums{k}", [128, NB, 2]) for k in range(RING)]
    diff, sqdiff, mean, var_sum, root, rstd, shift_row = (
        [sb(f"{n}{k}", [128, NB, 1]) for k in range(RING)]
        for n in ("diff", "sqdiff", "mean", "var_sum", "root", "rstd", "shift_row"))
    eps = sb("eps", [128, 1])
    warm = sb("warm", [128, 1])
    ones = sb("ones2", [128, 128])
    diag_scale, diag_shift = sb("diag_scale", [128, D]), sb("diag_shift", [128, D])
    shift_all = sb("shift_all", [128, 1, D])
    bst = [sb(f"bst{n}", [128, CHUNKS, 6]) for n in range(3)]
    bmv = sb("bmv", [128, 3, 2])
    broot, brs, scale, mshift, shift = (sb(n, [128, 3, 1]) for n in ("broot", "brs", "scale", "mshift", "shift"))

    xr_in = [sem(f"xr_in{k}") for k in range(SLOTS)]
    stored = [sem(f"stored{k}") for k in range(RING)]
    ones_made = sem("ones2_made")
    centred = sem("centred")
    eps_made, bn_root, bn_step, bn1_done, bn2_done = (sem(n) for n in ("eps_made", "bn_root", "bn_step", "bn1_done", "bn2_done"))
    hsum_out, hT_made, res_out = (sem(n) for n in ("hsum_out", "hT_made", "res_out"))
    x1_kept = [sem(f"x1_kept{k}") for k in range(SLOTS)]
    st_out, sums_out, sqdiff_out, var_out, root_out, rstd_out, shift_out, part_a, part_b = (
        sem(n) for n in ("st_out", "sums_out", "sqdiff_out", "var_out", "ln_root_out", "rstd_out", "shift_out", "part_a", "part_b"))
    agg_made, agg_out, hid_made, hid_out, bst_out = (sem(n) for n in ("agg2_made", "agg2_out", "hid_made", "hid_out", "bst_out"))
    hh_out, o_made, o_out, ost_out = (sem(n) for n in ("hh_out", "o_made", "o_out", "ost_out"))
    diags_made, shift_all_made, shift_all_out, plus_out, mix_made = (
        sem(n) for n in ("diags_made", "shift_all_made", "shift_all_out", "plus_out", "mix_made"))

    TURN, LN, LN_END, AGG, HIDDEN, STATS = 0, 1, 2, 3, 5, 7
    START, END_DVE, END_ACT = 1, 2, 3

    def ln_stats(dve, c, past, k, rows):
        for b in range(NB):
            last = nc.vector.bn_stats(st[k][:, b, :], rows(b))
        last.then_inc(st_out, 1)

    def ln_sums(dve, c, past, k):
        dve.wait_ge(st_out, c + (past + 1))
        nc.vector.tensor_tensor(sums[k][:, :, :], st[k][:, :, 1:3], st[k][:, :, 4:6], ALU.add)
        nc.vector.tensor_tensor(diff[k][:, :, 0], st[k][:, :, 1], st[k][:, :, 4], ALU.subtract).then_inc(sums_out, 1)

    def ln_mean(dve, c, past, k):
        dve.wait_ge(sums_out, c + (past + 1))
        nc.vector.tensor_scalar(mean[k][:, :, 0], sums[k][:, :, 0], 0.5, None, ALU.mult)
        nc.vector.scalar_tensor_tensor(out=sqdiff[k][:, :, 0], in0=diff[k][:, :, 0], scalar=D / 4, in1=diff[k][:, :, 0],
                                       op0=ALU.mult, op1=ALU.mult).then_inc(sqdiff_out, 1)

    def ln_var(dve, c, past, k):
        dve.wait_ge(sqdiff_out, c + (past + 1))
        nc.vector.tensor_tensor(var_sum[k][:, :, 0], sqdiff[k][:, :, 0], sums[k][:, :, 1], ALU.add).then_inc(var_out, 1)

    def ln_root(act, c, past, k):
        act.wait_ge(var_out, c + (past + 1))
        nc.scalar.activation(root[k][:, :, 0], var_sum[k][:, :, 0], ACT.Sqrt, bias=eps[:, 0:1], scale=1.0 / D).then_inc(root_out, 1)

    def ln_rstd(dve, c, past, k):
        dve.wait_ge(root_out, c + (past + 1))
        nc.vector.reciprocal(rstd[k][:, :, 0], root[k][:, :, 0]).then_inc(rstd_out, 1)

    def ln_shift(dve, c, past, k):
        dve.wait_ge(rstd_out, c + (past + 1))
        nc.vector.scalar_tensor_tensor(out=shift_row[k][:, :, 0], in0=mean[k][:, :, 0], scalar=-1.0, in1=rstd[k][:, :, 0],
                                       op0=ALU.mult, op1=ALU.mult).then_inc(shift_out, 1)

    def ln_by_act(act, c, past, k, rows, target, batches):
        act.wait_ge(shift_out, c + (past + 1))
        for b in batches:
            last = nc.scalar.activation(target[:, b, :], rows(b), ACT.Identity, bias=shift_row[k][:, b, :],
                                        scale=rstd[k][:, b, :])
        last.then_inc(part_a, 1)

    def ln_by_dve(k, rows, target, batches):
        for b in batches:
            last = nc.vector.tensor_scalar(target[:, b, :], rows(b), mean[k][:, b, 0:1], rstd[k][:, b, 0:1],
                                           ALU.subtract, ALU.mult)
        last.then_inc(part_b, 1)

    def res_rows(k):
        return lambda b: res[k][:, b, :]

    def mix_bank(ring):
        return bank[RING + ring]

    def mix_rows(ring):
        return lambda b: mix_bank(ring)[:, b * D:(b + 1) * D]

    ACT1, POOL1 = range(0, 3), range(3, NB)
    ACT3, DVE3 = range(0, 3), range(3, NB)

    def batch_norm(dve, count, which, gain, bias, done):
        lo, hi = which[0], which[-1] + 1
        for n in which:
            last = nc.vector.bn_aggr(bmv[:, n, :], bst[n][:, :, :].rearrange("p c s -> p (c s)"))
        last.then_inc(bn_step, 1)
        dve.wait_ge(bn_root, count // 4 + 1)
        nc.vector.reciprocal(brs[:, lo:hi, 0], broot[:, lo:hi, 0]).then_inc(bn_step, 1)
        dve.wait_ge(bn_step, count + 2)
        nc.vector.tensor_tensor(scale[:, lo:hi, 0], brs[:, lo:hi, 0], gain, ALU.mult).then_inc(bn_step, 1)
        dve.wait_ge(bn_step, count + 3)
        nc.vector.tensor_tensor(mshift[:, lo:hi, 0], bmv[:, lo:hi, 0], scale[:, lo:hi, 0], ALU.mult).then_inc(bn_step, 1)
        dve.wait_ge(bn_step, count + 4)
        nc.vector.tensor_tensor(shift[:, lo:hi, 0], bias, mshift[:, lo:hi, 0], ALU.subtract).then_inc(done, 1)

    def columns(c):
        return bass.ds(c * COLS, COLS)

    def batches_of(c):
        return bass.ds(c * NB, NB)

    with nc.Block() as block:
        @block.sync
        def _(sp):
            def keep(c, k):
                sp.wait_ge(part_a, c + 1)
                sp.wait_ge(part_b, c + 1)
                sp.dma_start(x1[:, batches_of(c), :], normed[k][:, :, :]).then_inc(x1_kept[k], 16)

            for k in range(SLOTS):
                sp.dma_start(xr[k][:, :, :], x_v[:, k * NB:(k + 1) * NB, :]).then_inc(xr_in[k], 16)
            with sp.Fori(SLOTS, CHUNKS - SLOTS + 1, SLOTS) as c:
                for k in range(SLOTS):
                    sp.wait_ge(res_out, c + (k - SLOTS + 1))
                    sp.dma_start(xr[k][:, :, :], x_v[:, batches_of(c + k), :]).then_inc(xr_in[k], 16)
                    keep(c + (k - SLOTS), k)
            for c in range(CHUNKS - SLOTS, CHUNKS):
                keep(c, c % SLOTS)
            with sp.Fori(0, CHUNKS - RING + 1, RING) as c:
                for k in range(RING):
                    sp.wait_ge(part_a, c + (CHUNKS + k + 1))
                    sp.wait_ge(part_b, c + (CHUNKS + k + 1))
                    sp.dma_start(out_v[:, batches_of(c + k), :], normed[k][:, :, :]).then_inc(stored[k], 16)
            for k in range(RING):
                sp.wait_ge(stored[k], 16 * (CHUNKS // RING) + 16)

        @block.gpsimd
        def _(pool):
            for k in range(RING):
                pool.sem_inc(stored[k], 16)
            nc.gpsimd.memset(eps[:, :], EPS).then_inc(eps_made, 1)
            nc.gpsimd.memset(ones[:, :], 1.0).then_inc(ones_made, 1)

            def first_pass(j, n):
                c, k = at_chunk(j, TURN), n % SLOTS
                if c is not None:
                    need(pool, hT_made, c + (1 - SLOTS))
                    nc.gpsimd.tensor_tensor(h_sum[k][:, :, :].rearrange("p b t -> p t b"), H_hi[:, :, batches_of(c)].bitcast(F32),
                                            H_lo[:, :, batches_of(c)].bitcast(F32), ALU.add).then_inc(hsum_out, 1)
                c, k = at_chunk(j, LN_END), (n - LN_END) % SLOTS
                if c is not None:
                    pool.wait_ge(shift_out, c + 1)
                    mine = slice(POOL1.start, POOL1.stop)
                    shape = [128, len(POOL1), D]
                    nc.gpsimd.tensor_tensor(normed[k][:, mine, :], res[k][:, mine, :], mean[k][:, mine, :].to_broadcast(shape),
                                            ALU.subtract).then_inc(centred, 1)
                    pool.wait_ge(centred, c + 1)
                    nc.gpsimd.tensor_tensor(normed[k][:, mine, :], normed[k][:, mine, :], rstd[k][:, mine, :].to_broadcast(shape),
                                            ALU.mult).then_inc(part_b, 1)

            def plus_shift(c, n):
                k = n % SLOTS
                need(pool, mix_made, c + (1 - SLOTS))
                nc.gpsimd.tensor_tensor(x1_plus[k][:, :, :], x1[:, batches_of(c), :],
                                        shift_all[:, :, :].to_broadcast([128, NB, D]), ALU.add).then_inc(plus_out, 1)

            pipelined(pool, LN_END, SLOTS, first_pass)
            pool.wait_ge(hT_made, CHUNKS)
            for k in range(SLOTS):
                pool.wait_ge(x1_kept[k], 16 * (CHUNKS // SLOTS))
            pool.wait_ge(shift_all_out, 1)
            pipelined(pool, 0, SLOTS, plus_shift)

        @block.tensor
        def _(pe):
            def first_pass(j, n):
                c, k = at_chunk(j, HIDDEN), (n - HIDDEN) % SLOTS
                if c is not None:
                    pe.wait_ge(agg_out, c + 1)
                    need(pe, hid_out, c + (1 - SLOTS))
                    for h in range(HALVES):
                        last = nc.tensor.matmul(bank[4 + 2 * k + h][:, :], w1T[:, h, :], agg[k], start=True, stop=True)
                    last.then_inc(hid_made, 1)
                c, k = at_chunk(j, TURN), (n - TURN) % SLOTS
                if c is not None:
                    pe.wait_ge(hsum_out, c + 1)
                    need(pe, res_out, c + (1 - SLOTS))
                    for b in range(NB):
                        last = nc.tensor.transpose(bank[k][:, b * D:(b + 1) * D], h_sum[k][:, b, :], ident[:, :])
                    last.then_inc(hT_made, 1)
                c, k = at_chunk(j, AGG), (n - AGG) % SLOTS
                if c is not None:
                    pe.wait_ge(part_a, c + 1)
                    pe.wait_ge(part_b, c + 1)
                    need(pe, agg_out, c + (1 - SLOTS))
                    for b in range(NB):
                        last = nc.tensor.matmul(bank[2 + k][:, b * T:(b + 1) * T], normed[k][:, b, :], a_hatT[:, :], start=True, stop=True)
                    last.then_inc(agg_made, 1)

            def second_pass(c, n):
                k = n % SLOTS
                need(pe, o_out, c + (1 - SLOTS))
                for h in range(HALVES):
                    pe.wait_ge(hh_out, c * HALVES + (h + 1))
                    last = nc.tensor.matmul(bank[k][:, :], w2T[:, h, :], hh[k][:, h, :], start=h == 0, stop=h == HALVES - 1)
                last.then_inc(o_made, 1)

            def third_pass(c):
                ring, k = c % RING, c % SLOTS
                need(pe, part_a, c + (CHUNKS + 1 - RING))
                need(pe, part_b, c + (CHUNKS + 1 - RING))
                for b in range(NB):
                    nc.tensor.matmul(mix_rows(ring)(b), o_all[:, c * COLS + b * T:c * COLS + (b + 1) * T], diag_scale[:, :], start=b == 0, stop=False)
                pe.wait_ge(plus_out, c + 1)
                nc.tensor.matmul(mix_bank(ring)[:, :], ident[:, :], x1_plus[k][:, :, :].rearrange("p b d -> p (b d)"),
                                 start=False, stop=True).then_inc(mix_made, 1)

            pipelined(pe, HIDDEN, SLOTS, first_pass)
            pipelined(pe, 0, SLOTS, second_pass)
            pe.wait_ge(ones_made, 1)
            pe.wait_ge(diags_made, 1)
            nc.tensor.matmul(bank[2][:, 0:D], ones[:, :], diag_shift[:, :], start=True, stop=True).then_inc(shift_all_made, 1)
            for c in range(CHUNKS):
                third_pass(c)

        @block.scalar
        def _(act):
            act.wait_ge(eps_made, 1)
            nc.scalar.activation(warm[:, :], eps[:, :], ACT.Sqrt)

            def first_pass(j, n):
                c, k = at_chunk(j, HIDDEN), (n - HIDDEN) % SLOTS
                if c is not None:
                    act.wait_ge(hid_made, c + 1)
                    for h in range(HALVES):
                        last = nc.scalar.activation(hid[h][:, columns(c)], bank[4 + 2 * k + h][:, :],
                                                    ACT.Identity, bias=cols[:, ROW_B1 + h:ROW_B1 + h + 1])
                    last.then_inc(hid_out, 1)
                c, k = at_chunk(j, LN_END), (n - LN_END) % SLOTS
                if c is not None:
                    ln_by_act(act, c, 0, k, res_rows(k), normed[k], ACT1)
                c, k = at_chunk(j, AGG), (n - AGG) % SLOTS
                if c is not None:
                    act.wait_ge(agg_made, c + 1)
                    nc.scalar.copy(agg[k], bank[2 + k][:, :]).then_inc(agg_out, 1)
                c, k = at_chunk(j, LN), (n - LN) % SLOTS
                if c is not None:
                    ln_root(act, c, 0, k)

            def second_pass(c, n):
                k = n % SLOTS
                need(act, o_made, c + (1 - SLOTS))
                for h in range(HALVES):
                    nc.scalar.activation(hh[k][:, h, :], hid[h][:, columns(c)],
                                         ACT.Relu, bias=shift[:, h, :], scale=scale[:, h, :]).then_inc(hh_out, 1)

            def third_pass(j, n):
                c, ring = at_chunk(j, END_ACT), (n - END_ACT) % RING
                if c is not None:
                    act.wait_ge(part_b, c + (CHUNKS + 1))
                    ln_by_act(act, c, CHUNKS, ring, mix_rows(ring), normed[ring], ACT3)
                c, ring = at_chunk(j, START), (n - START) % RING
                if c is not None:
                    ln_root(act, c, CHUNKS, ring)

            pipelined(act, HIDDEN, SLOTS, first_pass)
            act.wait_ge(bn_step, 1)
            nc.scalar.activation(broot[:, 0:2, 0], bmv[:, 0:2, 1], ACT.Sqrt, bias=eps[:, 0:1]).then_inc(bn_root, 1)
            act.wait_ge(bn1_done, 1)
            pipelined(act, 0, SLOTS, second_pass)
            act.wait_ge(bn_step, 5)
            nc.scalar.activation(broot[:, 2:3, 0], bmv[:, 2:3, 1], ACT.Sqrt, bias=eps[:, 0:1]).then_inc(bn_root, 1)
            act.wait_ge(shift_all_made, 1)
            nc.scalar.copy(shift_all[:, 0, :], bank[2][:, 0:D]).then_inc(shift_all_out, 1)
            pipelined(act, END_ACT, RING, third_pass)

        @block.vector
        def _(dve):
            def first_pass(j, n):
                start, k = at_chunk(j, LN), (n - LN) % SLOTS
                end, e = at_chunk(j, LN_END), (n - LN_END) % SLOTS
                stats = at_chunk(j, STATS)

                def hidden_stats(h):
                    if stats is not None:
                        ins = nc.vector.bn_stats(bst[h][:, bass.ds(stats, 1), :].rearrange("p c s -> p (c s)"), hid[h][:, columns(stats)])
                        if h == HALVES - 1:
                            ins.then_inc(bst_out, 1)

                if stats is not None:
                    dve.wait_ge(hid_out, stats + 1)
                hidden_stats(0)
                if end is not None:
                    need(dve, x1_kept[e], (end - e) * (16 // SLOTS))
                    need(dve, agg_made, end + (1 - SLOTS))
                    ln_rstd(dve, end, 0, e)
                if start is not None:
                    dve.wait_ge(hT_made, start + 1)
                    dve.wait_ge(xr_in[k], (start - k) * (16 // SLOTS) + 16)
                    need(dve, part_a, start + (1 - SLOTS))
                    need(dve, part_b, start + (1 - SLOTS))
                    nc.vector.tensor_tensor(res[k][:, :, :], bank[k][:, :].rearrange("p (b d) -> p b d", b=NB),
                                            xr[k][:, :, :], ALU.add).then_inc(res_out, 1)
                if end is not None:
                    ln_shift(dve, end, 0, e)
                if start is not None:
                    dve.wait_ge(res_out, start + 1)
                    ln_stats(dve, start, 0, k, res_rows(k))
                    ln_sums(dve, start, 0, k)
                hidden_stats(1)
                if start is not None:
                    ln_mean(dve, start, 0, k)
                    ln_var(dve, start, 0, k)

            def second_pass(c, n):
                k = n % SLOTS
                dve.wait_ge(o_made, c + 1)
                nc.vector.tensor_scalar(o_all[:, columns(c)], bank[k][:, :], cols[:, ROW_B2:ROW_B2 + 1], None, ALU.add).then_inc(o_out, 1)
                dve.wait_ge(o_out, c + 1)
                nc.vector.bn_stats(bst[2][:, bass.ds(c, 1), :].rearrange("p c s -> p (c s)"), o_all[:, columns(c)]).then_inc(ost_out, 1)

            def third_pass(j, n):
                start, k = at_chunk(j, START), (n - START) % RING
                end, e = at_chunk(j, END_DVE), (n - END_DVE) % RING
                if start is not None:
                    dve.wait_ge(mix_made, start + 1)
                    ln_stats(dve, start, CHUNKS, k, mix_rows(k))
                if end is not None:
                    ln_rstd(dve, end, CHUNKS, e)
                if start is not None:
                    ln_sums(dve, start, CHUNKS, k)
                if end is not None:
                    dve.wait_ge(stored[e], (end - e) * (16 // RING) + 16)
                    ln_shift(dve, end, CHUNKS, e)
                if start is not None:
                    ln_mean(dve, start, CHUNKS, k)
                if end is not None:
                    ln_by_dve(e, mix_rows(e), normed[e], DVE3)
                if start is not None:
                    ln_var(dve, start, CHUNKS, k)

            pipelined(dve, STATS, SLOTS, first_pass)
            dve.wait_ge(bst_out, CHUNKS)
            batch_norm(dve, 0, [0, 1], cols[:, ROW_G1:ROW_G1 + 2], cols[:, ROW_BE1:ROW_BE1 + 2], bn1_done)
            pipelined(dve, 0, SLOTS, second_pass)
            dve.wait_ge(ost_out, CHUNKS)
            batch_norm(dve, 4, [2], cols[:, ROW_G2:ROW_G2 + 1], cols[:, ROW_BE2:ROW_BE2 + 1], bn2_done)
            dve.wait_ge(bn2_done, 1)
            nc.vector.tensor_scalar(diag_scale[:, :], ident[:, :], scale[:, 2, :], None, ALU.mult)
            nc.vector.tensor_scalar(diag_shift[:, :], ident[:, :], shift[:, 2, :], None, ALU.mult).then_inc(diags_made, 1)
            for k in range(SLOTS):
                dve.wait_ge(x1_kept[k], 16 * (CHUNKS // SLOTS))
            pipelined(dve, END_DVE, RING, third_pass)


_INS = ["x", "adj", "L0_gnn_Wg0", "L0_gnn_bg0", "L0_gnn_Wg1", "L0_gnn_bg1", "L0_gnn_Wih", "L0_gnn_Whh", "L0_gnn_bih",
        "L0_gnn_bhh", "L1_gnn_W1", "L1_gnn_b1", "L1_gnn_g1", "L1_gnn_be1", "L1_gnn_W2", "L1_gnn_b2", "L1_gnn_g2",
        "L1_gnn_be2"]


def kernel(**inputs):
    import numpy as _np
    import concourse.bacc as _bacc
    from concourse import mybir as _mybir
    from concourse.bass_utils import run_bass_kernel_spmd as _run

    nc = _bacc.Bacc("TRN2", target_bir_lowering=False, num_devices=1)
    arrays, args = {}, []
    for name in _INS:
        a = _np.ascontiguousarray(inputs[name])
        arrays[f"in_{name}_dram"] = a
        args.append(nc.dram_tensor(f"in_{name}_dram", a.shape, _mybir.dt.from_np(a.dtype), kind="ExternalInput").ap())
    args.append(nc.dram_tensor("out_dram", (B, T, D), _mybir.dt.float32, kind="ExternalOutput").ap())
    build(nc, *args)
    r = _run(nc, [arrays], core_ids=[0])
    return r.results[0]["out_dram"]
```
